# Optimizing a Trainium2 kernel written in Bass

```python
import numpy as np
import jax
import jax.numpy as jnp

def _softmax(x, axis=-1):
    return jax.nn.softmax(x, axis=axis)

def _gelu(x):
    return jax.nn.gelu(x, approximate=True)

def _silu(x):
    return jax.nn.silu(x)

def _sigmoid(x):
    return jax.nn.sigmoid(x)

def _layernorm(x, axis=-1, eps=1e-05):
    m = jnp.mean(x, axis=axis, keepdims=True)
    v = jnp.var(x, axis=axis, keepdims=True)
    return (x - m) / jnp.sqrt(v + eps)

def _scatter_add(tgt, idx, src, axis=0):
    return tgt.at[idx].add(src)

def _segment_sum(src, seg, n):
    return jax.ops.segment_sum(src, seg, n)
kernel_name = 'mk_decoder_postln_d1_seqx_r4_4069ca'

def setup_inputs(seed: int=0):
    np.random.seed(seed)
    _w = jnp.asarray

    def _rec_inputs():
        import jax
        import jax.numpy as jnp
        _rk = jax.random.key(seed)
        x = -0.0002928 + 1 * jax.random.normal(jax.random.fold_in(_rk, 1), (16, 256, 256), jnp.float32)
        _lenS = 256 - jax.random.randint(jax.random.fold_in(_rk, 7), (16,), 0, max(1, 256 // 4) + 1, jnp.int32)
        _lenS2 = 256 - jax.random.randint(jax.random.fold_in(_rk, 8), (16,), 0, max(1, 256 // 4) + 1, jnp.int32)
        _ctx_1024P = jax.random.normal(jax.random.fold_in(_rk, 11), (16, 16, 256), jnp.float32)
        _ctx_1024c = jax.random.dirichlet(jax.random.fold_in(_rk, 511), 0.3 * jnp.ones((16,), jnp.float32), (16, 256))
        _ctx_1024t = jnp.einsum('bsk,bkd->bsd', _ctx_1024c, _ctx_1024P)
        _ctx_1024t = _ctx_1024t * jax.lax.rsqrt(jnp.mean(jnp.square(_ctx_1024t)) + 1e-12) * 0.953939
        ctx_1024 = 2.81802e-05 + 1.00001 * (_ctx_1024t + 0.3 * jax.random.normal(jax.random.fold_in(_rk, 611), (16, 256, 256), jnp.float32))
        _validS = jnp.arange(256)[None, :] < _lenS[:, None]
        _validS2 = jnp.arange(256)[None, :] < _lenS2[:, None]
        _causal = jnp.tril(jnp.ones((256, 256), dtype=bool))
        mask_BxS2_bk1 = jnp.broadcast_to(_validS2[:, :], (16, 256))
        return (x, ctx_1024, mask_BxS2_bk1)
    x, ctx_1024, mask_BxS2_bk1 = _rec_inputs()

    def _L0_attn_setup():
        import jax, jax.numpy as jnp
        import numpy as np
        import math
        B_, S_, D_, R_, NC_, NK_, SD_, KK_ = (4, 512, 256, 128, 64, 8192, 64, 8)

        def _reference_tuple_inner(x, A, Bm, W_imp, W_router, compress, K, V):
            B, S, D = x.shape
            kk = KK_
            xB = jnp.einsum('bsd,de->sbe', x, Bm)

            def step(h, u):
                h = h @ A + u
                return (h, None)
            h0 = jnp.zeros((B, A.shape[0]), x.dtype)
            h_final, _ = jax.lax.scan(step, h0, xB)
            h_proj = h_final @ W_imp.T
            importance = jax.nn.softmax(jnp.einsum('bsd,bd->bs', x, h_proj), axis=-1)
            token_pref = jax.nn.softmax(jnp.einsum('bsd,nd->bsn', x, W_router), axis=-1)
            neuron_w = jnp.einsum('bs,bsn->bn', importance, token_pref)
            neuron_w = neuron_w / (neuron_w.sum(-1, keepdims=True) + 1e-08)
            shared_compress = jnp.einsum('bn,ndr->bdr', neuron_w, compress)
            Q = jnp.einsum('bsd,bdr->bsr', x, shared_compress)
            scores = jnp.einsum('bsr,nr->bsn', Q, K) / math.sqrt(K.shape[1])
            topk_scores, topk_idx = jax.lax.top_k(scores, kk)
            weights = jax.nn.softmax(topk_scores, axis=-1)
            selected_V = V[topk_idx]
            output = jnp.einsum('bskd,bsk->bsd', selected_V, weights)
            return (output, importance, neuron_w, topk_idx, weights)
        key = jax.random.key(seed)
        ks = jax.random.split(key, 8)
        return {'x': jax.random.normal(ks[0], (B_, S_, D_), jnp.float32), 'A': jax.random.normal(ks[1], (SD_, SD_), jnp.float32) * 0.01, 'Bm': jax.random.normal(ks[2], (D_, SD_), jnp.float32) * 0.01, 'W_imp': jax.random.normal(ks[3], (D_, SD_), jnp.float32) * 0.02, 'W_router': jax.random.normal(ks[4], (NC_, D_), jnp.float32) * 0.02, 'compress': jax.random.normal(ks[5], (NC_, D_, R_), jnp.float32) * (1.0 / math.sqrt(D_)), 'K': jax.random.normal(ks[6], (NK_, R_), jnp.float32) * 0.02, 'V': jax.random.normal(ks[7], (NK_, D_), jnp.float32) * 0.02}
    _L0_attn_all = _L0_attn_setup()
    _L0_attn_in = {k: v for k, v in _L0_attn_all.items() if k in ('A', 'Bm', 'W_imp', 'W_router', 'compress', 'K', 'V')}
    del _L0_attn_all

    def _L0_xattn_setup():
        import jax, jax.numpy as jnp
        import numpy as np
        B, N, M = (4, 256, 1024)
        DQ, DC = (256, 256)
        H, DH = (16, 64)
        INNER = H * DH
        SCALE = DH ** (-0.5)
        key = jax.random.key(seed)
        ks = jax.random.split(key, 6)
        x = jax.random.normal(ks[0], (B, N, DQ), dtype=jnp.float32)
        context = jax.random.normal(ks[1], (B, M, DC), dtype=jnp.float32)
        mask = jax.random.bernoulli(ks[2], 0.9, (B, M))
        Wq = jax.random.normal(ks[3], (DQ, INNER), dtype=jnp.float32) / np.sqrt(DQ)
        Wkv = jax.random.normal(ks[4], (DC, 2 * INNER), dtype=jnp.float32) / np.sqrt(DC)
        Wo = jax.random.normal(ks[5], (INNER, DQ), dtype=jnp.float32) / np.sqrt(INNER)
        bo = jnp.zeros((DQ,), dtype=jnp.float32)
        return {'x': x, 'context': context, 'mask': mask, 'Wq': Wq, 'Wkv': Wkv, 'Wo': Wo, 'bo': bo}
    _L0_xattn_all = _L0_xattn_setup()
    _L0_xattn_in = {k: v for k, v in _L0_xattn_all.items() if k in ('Wq', 'Wkv', 'Wo', 'bo')}
    del _L0_xattn_all

    def _L0_ffn_setup():
        import jax, jax.numpy as jnp
        import numpy as np
        DM = 256
        NEXPERTS = 32
        EXPERTSETS = 4
        EXPERTSIZE = 32
        BATCH, SEQ = (4, 512)
        key = jax.random.key(seed)
        k0, k1, k2, k3 = jax.random.split(key, 4)
        scale = 0.02
        x = jax.random.normal(k0, (BATCH, SEQ, DM), jnp.float32)
        controller = jax.random.normal(k1, (DM, NEXPERTS, EXPERTSETS), jnp.float32) * scale
        f1 = jax.random.normal(k2, (DM, NEXPERTS, EXPERTSETS, EXPERTSIZE), jnp.float32) * scale
        bias = jnp.zeros((NEXPERTS, EXPERTSETS, EXPERTSIZE), jnp.float32)
        f2 = jax.random.normal(k3, (NEXPERTS, EXPERTSETS, EXPERTSIZE, DM), jnp.float32) * scale
        return {'x': x, 'controller': controller, 'f1': f1, 'bias': bias, 'f2': f2}
    _L0_ffn_all = _L0_ffn_setup()
    _L0_ffn_in = {k: v for k, v in _L0_ffn_all.items() if k in ('controller', 'f1', 'bias', 'f2')}
    del _L0_ffn_all
    return {'x': x, 'ctx_1024': ctx_1024, 'mask_BxS2_bk1': mask_BxS2_bk1, 'L0_attn_A': _L0_attn_in['A'], 'L0_attn_Bm': _L0_attn_in['Bm'], 'L0_attn_W_imp': _L0_attn_in['W_imp'], 'L0_attn_W_router': _L0_attn_in['W_router'], 'L0_attn_compress': _L0_attn_in['compress'], 'L0_attn_K': _L0_attn_in['K'], 'L0_attn_V': _L0_attn_in['V'], 'L0_xattn_Wq': _L0_xattn_in['Wq'], 'L0_xattn_Wkv': _L0_xattn_in['Wkv'], 'L0_xattn_Wo': _L0_xattn_in['Wo'], 'L0_xattn_bo': _L0_xattn_in['bo'], 'L0_ffn_controller': _L0_ffn_in['controller'], 'L0_ffn_f1': _L0_ffn_in['f1'], 'L0_ffn_bias': _L0_ffn_in['bias'], 'L0_ffn_f2': _L0_ffn_in['f2']}

def reference(x, ctx_1024, mask_BxS2_bk1, L0_attn_A, L0_attn_Bm, L0_attn_W_imp, L0_attn_W_router, L0_attn_compress, L0_attn_K, L0_attn_V, L0_xattn_Wq, L0_xattn_Wkv, L0_xattn_Wo, L0_xattn_bo, L0_ffn_controller, L0_ffn_f1, L0_ffn_bias, L0_ffn_f2):
    import jax
    import jax.numpy as jnp

    def _L0_attn_ref(x, A, Bm, W_imp, W_router, compress, K, V):
        import jax, jax.numpy as jnp
        import numpy as np
        import math
        B_, S_, D_, R_, NC_, NK_, SD_, KK_ = (4, 512, 256, 128, 64, 8192, 64, 8)

        def _reference_tuple_inner(x, A, Bm, W_imp, W_router, compress, K, V):
            B, S, D = x.shape
            kk = KK_
            xB = jnp.einsum('bsd,de->sbe', x, Bm)

            def step(h, u):
                h = h @ A + u
                return (h, None)
            h0 = jnp.zeros((B, A.shape[0]), x.dtype)
            h_final, _ = jax.lax.scan(step, h0, xB)
            h_proj = h_final @ W_imp.T
            importance = jax.nn.softmax(jnp.einsum('bsd,bd->bs', x, h_proj), axis=-1)
            token_pref = jax.nn.softmax(jnp.einsum('bsd,nd->bsn', x, W_router), axis=-1)
            neuron_w = jnp.einsum('bs,bsn->bn', importance, token_pref)
            neuron_w = neuron_w / (neuron_w.sum(-1, keepdims=True) + 1e-08)
            shared_compress = jnp.einsum('bn,ndr->bdr', neuron_w, compress)
            Q = jnp.einsum('bsd,bdr->bsr', x, shared_compress)
            scores = jnp.einsum('bsr,nr->bsn', Q, K) / math.sqrt(K.shape[1])
            topk_scores, topk_idx = jax.lax.top_k(scores, kk)
            weights = jax.nn.softmax(topk_scores, axis=-1)
            selected_V = V[topk_idx]
            output = jnp.einsum('bskd,bsk->bsd', selected_V, weights)
            return (output, importance, neuron_w, topk_idx, weights)
        return _reference_tuple_inner(x, A, Bm, W_imp, W_router, compress, K, V)[0]

    def _L0_xattn_ref(x, context, mask, Wq, Wkv, Wo, bo):
        import jax, jax.numpy as jnp
        import numpy as np
        B, N, M = (4, 256, 1024)
        DQ, DC = (256, 256)
        H, DH = (16, 64)
        INNER = H * DH
        SCALE = DH ** (-0.5)
        q = x @ Wq
        kv = context @ Wkv
        k, v = jnp.split(kv, 2, axis=-1)

        def heads(t):
            b, s, _ = t.shape
            return t.reshape(b, s, H, DH).transpose(0, 2, 1, 3)
        q, k, v = (heads(q), heads(k), heads(v))
        sim = jnp.einsum('bhid,bhjd->bhij', q, k) * SCALE
        max_neg = -jnp.finfo(sim.dtype).max
        sim = jnp.where(mask[:, None, None, :], sim, max_neg)
        sim = jnp.clip(sim, -5.0, 5.0)
        attn = jax.nn.softmax(sim, axis=-1)
        out = jnp.einsum('bhij,bhjd->bhid', attn, v)
        out = out.transpose(0, 2, 1, 3).reshape(x.shape[0], x.shape[1], INNER)
        return out @ Wo + bo

    def _L0_ffn_ref(x, controller, f1, bias, f2):
        import jax, jax.numpy as jnp
        import numpy as np
        DM = 256
        NEXPERTS = 32
        EXPERTSETS = 4
        EXPERTSIZE = 32
        BATCH, SEQ = (4, 512)
        B, L, d = x.shape
        t = controller.shape[1]
        g = L // t
        grouped = x.reshape(B, g, t, d)
        logits = jnp.einsum('bgtd,des->bgtes', grouped, controller)
        tie = jnp.linspace(0.0, 1e-06, t, dtype=logits.dtype).reshape(t, 1, 1)
        logits = logits + tie
        perm = (logits == jnp.max(logits, axis=-3, keepdims=True)).astype(x.dtype)
        perm = jax.lax.stop_gradient(perm)
        dispatched = jnp.einsum('bgtd,bgtes->bgesd', grouped, perm)
        inner = jax.nn.relu(jnp.einsum('bgesd,desf->bgesf', dispatched, f1) + bias)
        intermediate = jnp.einsum('bgesf,esfd->bgesd', inner, f2)
        out = jnp.einsum('bgesd,bgtes->bgtd', intermediate, perm)
        return out.reshape(B, L, d)
    x = _layernorm(x + _L0_attn_ref(x, L0_attn_A, L0_attn_Bm, L0_attn_W_imp, L0_attn_W_router, L0_attn_compress, L0_attn_K, L0_attn_V), axis=-1)
    x = _layernorm(x + _L0_xattn_ref(x, ctx_1024, mask_BxS2_bk1, L0_xattn_Wq, L0_xattn_Wkv, L0_xattn_Wo, L0_xattn_bo), axis=-1)
    x = _layernorm(x + _L0_ffn_ref(x, L0_ffn_controller, L0_ffn_f1, L0_ffn_bias, L0_ffn_f2), axis=-1)
    return x

_drawn_inputs = setup_inputs


def setup_inputs(seed=0):
    import zlib

    import numpy as np

    out = dict(_drawn_inputs(seed))
    spreads = {'L0_xattn_bo': (0.0, 0.1), 'L0_ffn_bias': (0.0, 0.522)}
    factors = {'L0_attn_A': 8.0,
     'L0_attn_Bm': 8.0,
     'L0_attn_W_imp': 8.0,
     'L0_attn_W_router': 8.0,
     'L0_attn_compress': 6.649,
     'L0_attn_K': 6.651,
     'L0_attn_V': 6.578}
    for name, (base, spread) in spreads.items():
        noise = np.random.default_rng([zlib.crc32(name.encode()), seed]).standard_normal(out[name].shape)
        drawn = base * np.exp(spread * noise) if base else spread * noise
        out[name] = jnp.asarray(drawn.astype(out[name].dtype))
    for name, factor in factors.items():
        out[name] = (out[name] * factor).astype(out[name].dtype)
    return out
```

```python
from contextlib import ExitStack

import numpy as np
import concourse.bass as bass
from concourse import mybir

F32 = mybir.dt.float32
F32R = mybir.dt.float32r
U32 = mybir.dt.uint32
U8 = mybir.dt.uint8
ALU = mybir.AluOpType
ACT = mybir.ActivationFunctionType
AX = mybir.AxisListType.X

P = 128
B, S, D = 16, 256, 256
KT = D // P
TT = S // P
SD = 64
NC = 64
R = 128
NK = 8192
TOPK = 8
STW = 1024
CH = 1024
NCH = NK // CH
H, DH = 16, 64
INNER = H * DH
NP = H // 2
GT = 32
SLOTS = 128
F = 32
NG = B * S // GT
NT = B * S // P
NQ = SLOTS // 4
RAD = 16
EPS = 1e-5
K_SCALE = float(R) ** -0.5
A_SCALE = float(DH) ** -0.5
E_LO, E_HI = float(np.exp(np.float32(-5.0))), float(np.exp(np.float32(5.0)))

PRE_PE = {k: n + 1 for n, k in enumerate(("scan1", "scan2", "hproj", "imp_pe", "impT_pe", "nw_pe", "nws_pe"))}
PRE_DVE = {k: n + 1 for n, k in enumerate(("scan1_evac", "scan2_evac", "hm_evac", "imp_max", "imp_sm", "uw_done",
                                           "nw_evac", "nd_done"))}

J_K, J_V, J_X1, J_Q, J_PV, J_WO, JOBS = 0, 4, 8, 10, 14, 22, 24


def build(nc, x, xT, ctxT, mrow, mcol, A, AT, BmT, WimpT, WrT, comp, KmT, V, Wq, Wk, Wv, Wo, bo, ctrl, f1, fb, f2,
          ident, tie, cidx, out):
    scd = nc.dram_tensor("shared_compress", [B * KT, P * R], F32, kind="Internal").ap()
    x2d = nc.dram_tensor("x2_scratch", [B * S, D], F32, kind="Internal").ap()
    with ExitStack() as ctx:
        names = {}

        def sem(name):
            if name not in names:
                names[name] = ctx.enter_context(nc.semaphore(name))
            return names[name]

        def sb(stack, name, shape, dt=F32):
            return stack.enter_context(nc.sbuf_tensor(name, shape, dt))

        def ps(name, cols):
            return ctx.enter_context(nc.psum_tensor(name, [P, cols], F32))

        scp = [ps(f"score_bank{i}", CH) for i in range(2)]
        sp_ = [ps(f"sim_bank{i}", 512) for i in range(2)]
        pp = [ps(f"proj_bank{i}", 512) for i in range(2)]

        idn = sb(ctx, "identity", [P, P])
        neghalf = sb(ctx, "neghalf", [P, 2])

        main = ctx.enter_context(ExitStack())
        kh, kl = sb(main, "keysT_hi", [P, NK], F32R), sb(main, "keysT_lo", [P, NK], F32R)
        wh, wl = sb(main, "wqkv_hi", [P, 3, KT, INNER], F32R), sb(main, "wqkv_lo", [P, 3, KT, INNER], F32R)
        wo = sb(main, "wo", [P, NP, D])
        bob = sb(main, "bo_bcast", [P, D])
        mcu = sb(main, "mask_col_u8", [P, KT, B], U8)
        mv = sb(main, "mask_weight", [P, KT, B])
        cix = sb(main, "chunk_offset", [P, 2, NCH * 8])

        pre = main.enter_context(ExitStack())
        xTa = sb(pre, "xT_all_", [P, KT, B * S])
        stg = [sb(pre, f"stage_{i}", [P, STW]) for i in range(2)]
        pw = sb(pre, "A_pow", [SD, RAD + 1, SD])
        qw = sb(pre, "A16_pow", [SD, RAD + 1, SD])
        tpw = [sb(pre, f"AT_pow{i}", [SD, SD]) for i in range(8)]
        bmt = sb(pre, "Bm_T", [SD, D])
        wit = sb(pre, "Wimp_T", [SD, D])
        wrt = sb(pre, "Wrouter_T", [P, KT, NC])
        ba = sb(pre, "Bm_A_pow", [P, KT, RAD, SD])
        gt = sb(pre, "scan_partial", [SD, B, RAD])
        ht = sb(pre, "h_final_T", [SD, B])
        hm = sb(pre, "h_proj_diag", [P, KT, B, B])
        impe = sb(pre, "importance", [B, S])
        imx = sb(pre, "imp_small", [B, 4])
        rte = sb(pre, "router_exp", [P, NT, NC])
        rmx = sb(pre, "router_max", [P, NT])
        rsm = sb(pre, "router_sum", [P, NT])
        uw = sb(pre, "token_weight", [P, NT])
        nw = sb(pre, "neuron_w", [NC, 3, B])
        ones = sb(pre, "ones64", [NC, NC])
        nd = sb(pre, "neuron_diag", [P, B, KT])
        cst = [sb(pre, f"comp_stage_{i}", [P, STW]) for i in range(2)]
        scs = [ba[0:B * KT, i, 0:512 // SD, :].rearrange("p a b -> p (a b)") for i in range(2)]
        pre.close()

        work = main.enter_context(ExitStack())
        xt = sb(work, "xT_in", [P, KT, S])
        xth, xtl = sb(work, "xT_hi", [P, KT, S], F32R), sb(work, "xT_lo", [P, KT, S], F32R)
        xn = sb(work, "x_in", [P, TT, D])
        sct = sb(work, "sc_in", [P, KT, R])
        sch, scl = sb(work, "sc_hi", [P, KT, R], F32R), sb(work, "sc_lo", [P, KT, R], F32R)
        qth, qtl = sb(work, "qT_hi", [P, S], F32R), sb(work, "qT_lo", [P, S], F32R)
        cv = sb(work, "cand_val", [P, TT, NCH * 8])
        ci = sb(work, "cand_idx", [P, TT, NCH * 8], U32)
        cf = sb(work, "cand_idx_f", [P, NCH * 8])
        v8 = sb(work, "top_val", [P, TT, TOPK])
        p8 = sb(work, "top_pos", [P, TOPK], U32)
        eqf = sb(work, "pos_onehot", [P, TOPK * NCH * 8])
        eq = eqf[:, :].rearrange("p (k c) -> p k c", k=TOPK)
        i8 = sb(work, "top_idx", [P, TT, TOPK], U32)
        nb = sb(work, "neg_max", [P, TT])
        w8 = sb(work, "top_weight", [P, TT, TOPK])
        wsum = sb(work, "weight_sum", [P, TT, 2])
        vg = sb(work, "v_rows", [P, TOPK, D])
        rd, acc = eqf[:, 0:S], eqf[:, S:S + D]
        st = sb(work, "ln_stats", [P, 6 * TT])
        ag = sb(work, "ln_aggr", [P, 2 * TT])
        ve = sb(work, "ln_var", [P, TT])
        rs = sb(work, "ln_rstd", [P, TT])
        x1 = sb(work, "x1", [P, TT, D])
        x1r = sb(work, "x1_residual", [P, TT, D])
        x1h, x1l = sb(work, "x1T_hi", [P, KT, S], F32R), sb(work, "x1T_lo", [P, KT, S], F32R)
        ct = sb(work, "ctxT_in", [P, KT, S])
        mr = sb(work, "mask_row", [P, S], U8)
        cm = sb(work, "ctxT_masked", [P, KT, S])
        cmh, cml = sb(work, "ctxm_hi", [P, KT, S], F32R), sb(work, "ctxm_lo", [P, KT, S], F32R)
        cth, ctl = sb(work, "ctx_hi", [P, KT, S], F32R), sb(work, "ctx_lo", [P, KT, S], F32R)
        kt = sb(work, "kT", [P, NP, S])
        qz = sb(work, "qT_padded", [P, H, S])
        vv = sb(work, "v", [P, KT, INNER])
        mb = sb(work, "mask_weight_b", [P, KT, DH])
        ex = [sb(work, f"exp{i}", [P, KT, S]) for i in range(4)]
        ot = kt
        z2 = x1r
        main.close()

        exl = ctx.enter_context(ExitStack())
        U = 4
        dtt = sb(exl, "dispatchedT", [P, KT, SLOTS, NG])
        pma = sb(exl, "permT_all", [P, B * S])
        ctr = sb(exl, "controller", [P, KT, SLOTS])
        tiet = sb(exl, "tie", [P, GT])
        fbt = sb(exl, "ffn_bias", [P, NQ])
        d1 = exl.enter_context(ExitStack())
        xb = [sb(d1, f"x2_tile{u}", [P, D]) for u in range(U)]
        xbt = [sb(d1, f"x2T_tile{u}", [P, KT, P]) for u in range(U)]
        lg = [sb(d1, f"logits{u}", [P, 4, GT]) for u in range(U)]
        mx = [sb(d1, f"logit_max{u}", [P, 4]) for u in range(U)]
        pm = [sb(d1, f"permT{u}", [P, 4, GT]) for u in range(U)]
        bd = [sb(d1, f"perm_diag{u}", [P, 4, SLOTS]) for u in range(U)]
        d1.close()
        d2 = exl.enter_context(ExitStack())
        f1q = [sb(d2, f"f1_quad{u}", [P, KT, P]) for u in range(2)]
        f2q = [sb(d2, f"f2_quad{u}", [P, D]) for u in range(2)]
        hb = [sb(d2, f"hidden_diag{u}", [P, 4, NG]) for u in range(2)]
        d2.close()
        d3 = exl.enter_context(ExitStack())
        xc = [sb(d3, f"x2_again{u}", [P, D]) for u in range(2)]
        gi = [sb(d3, f"group_inter{u}", [P, KT, 4, SLOTS]) for u in range(2)]
        pms = [sb(d3, f"permT_static{u}", [P, P]) for u in range(2)]
        it_ = [sb(d3, f"inter{u}", [P, 4, D]) for u in range(2)]
        zz = [sb(d3, f"x3_sum{u}", [P, D]) for u in range(2)]
        st3 = [sb(d3, f"stats3_{u}", [P, 6]) for u in range(2)]
        ag3 = [sb(d3, f"aggr3_{u}", [P, 2]) for u in range(2)]
        ve3 = [sb(d3, f"var3_{u}", [P, 1]) for u in range(2)]
        rs3 = [sb(d3, f"rstd3_{u}", [P, 1]) for u in range(2)]
        oo = [sb(d3, f"out_tile{u}", [P, D]) for u in range(2)]
        d3.close()

        V_rows = V
        scd_v = scd.rearrange("(b k) (p r) -> b p k r", k=KT, r=R)
        xn_v = x.rearrange("(b t p) d -> b p t d", p=P, t=TT)
        x2_v = x2d.rearrange("(b t p) d -> b p t d", p=P, t=TT)
        x2_t = x2d.rearrange("(n p) d -> n p d", p=P)
        out_t = out.rearrange("(n p) d -> n p d", p=P)

        block = ctx.enter_context(nc.Block())

        spare = {}

        def wait_apart(eng, name, v):
            if not isinstance(v, int):
                if eng not in spare:
                    spare[eng] = eng.alloc_register("wait_value")
                eng.reg_mov(spare[eng], v)
                v = spare[eng]
            eng.wait_ge(sem("v_const"), 1)
            eng.wait_ge(sem(name), v)

        PRIMED = ("proj_free0", "proj_free1", "exp_done", "cm_lo", "ctx_lo")

        def prime(eng, *which):
            for name in which:
                eng.sem_inc(sem(name), 1)

        class Turn:

            def __init__(self, c, attn, cross):
                self.c, self.attn, self.cross = c, attn, cross
                self.a = c + 1

            def w(self, eng, name, per, k, of, apart=False):
                v = of * per + k + (name in PRIMED)
                if isinstance(v, int) and v <= (name in PRIMED):
                    return
                if apart:
                    wait_apart(eng, name, v)
                else:
                    eng.wait_ge(sem(name), v)

        def turns(eng, body):
            body(Turn(-1, True, False))
            with eng.Fori(0, B - 1) as c:
                body(Turn(c, True, True))
            body(Turn(B - 1, False, True))

        def job_free(eng, t, j):
            t.w(eng, f"proj_free{j % 2}", JOBS // 2, j // 2, t.c)

        def job_full(eng, t, j):
            t.w(eng, f"proj_full{j % 2}", JOBS // 2, j // 2 + 1, t.c)

        def job_done(eng, t, j):
            t.w(eng, f"proj_free{j % 2}", JOBS // 2, j // 2 + 1, t.c)

        def apart(eng):
            eng.wait_ge(sem("v_const"), 1)

        STAGES = [(KmT, c, kh[:, c * STW:(c + 1) * STW], kl[:, c * STW:(c + 1) * STW]) for c in range(NK // STW)]
        STAGES += [(w, k, wh[:, n, k, :], wl[:, n, k, :]) for n, w in enumerate((Wq, Wk, Wv)) for k in range(KT)]
        NCS = P * R // STW

        @block.sync
        def _(sp):
            for dst, src in ((pw[:, 1, :], A), (tpw[0][:, :], AT), (bmt[:, :], BmT), (wit[:, :], WimpT),
                             (pw[:, 0, :], ident[0:SD, 0:SD]), (qw[:, 0, :], ident[0:SD, 0:SD]), (idn[:, :], ident)):
                sp.dma_start(dst, src).then_inc(sem("small_in"), 16)
            for q in range(4):
                n = B * S // 4
                sp.dma_start(xTa[:, :, q * n:(q + 1) * n], xT[:, :, q * n:(q + 1) * n]).then_inc(sem("xTa_in"), 16)
            sp.dma_start(wrt[:, :, :], WrT).then_inc(sem("xTa_in"), 16)
            for n in range(2):
                sp.dma_start(cst[n % 2][:, :], comp[:, n * STW:(n + 1) * STW]).then_inc(sem(f"comp_in{n % 2}"), 16)
            for n in range(32):
                m = n // 2 + 1
                if n >= 2 and n % 2 == 0 and m < NCS:
                    sp.wait_ge(sem("comp_used"), 2 * (m - 1))
                    sp.dma_start(cst[m % 2][:, :], comp[:, m * STW:(m + 1) * STW]).then_inc(sem(f"comp_in{m % 2}"), 16)
                sp.wait_ge(sem("sc_evac"), n + 1)
                sp.dma_start(scd[:, n * 512:(n + 1) * 512], scs[n % 2]).then_inc(sem(f"sc_store{n % 2}"), 16)
            sp.wait_ge(sem("sc_store0"), 256)
            sp.wait_ge(sem("sc_store1"), 256)
            sp.wait_ge(sem("stage_split"), len(STAGES))
            sp.wait_ge(sem("stage_hi"), len(STAGES))

            def body(t):
                if t.attn:
                    t.w(sp, "x_lo", 1, 0, t.a)
                    sp.dma_start(xt[:, :, :], xT[:, :, bass.ts(t.a, S)]).then_inc(sem("xt_in"), 16)
                    t.w(sp, "sc_lo", 1, 0, t.a)
                    sp.dma_start(sct[:, :, :], scd_v[t.a]).then_inc(sem("sct_in"), 16)
                if t.cross:
                    t.w(sp, "ctx_lo", 1, 0, t.c)
                    sp.dma_start(ct[:, :, :], ctxT[:, :, bass.ts(t.c, S)]).then_inc(sem("ct_in"), 16)
                    sp.dma_start(mr[:, :], mrow[t.c]).then_inc(sem("mr_in"), 16)
                if t.attn:
                    t.w(sp, "sum_done", TT, 0, t.a)
                    sp.dma_start(xn[:, :, :], xn_v[t.a]).then_inc(sem("xn_in"), 16)

            turns(sp, body)

            sp.wait_ge(sem("x2_stored"), 16 * B)
            sp.dma_start(ctr[:, :, :], ctrl).then_inc(sem("e_const"), 16)
            sp.dma_start(tiet[:, :], tie).then_inc(sem("e_const"), 16)
            sp.dma_start(fbt[:, :], fb).then_inc(sem("e_const"), 16)
            with sp.Fori(0, NT // U) as i:
                for u in range(U):
                    sp.wait_ge(sem("disp_pe"), i * U + 1)
                    sp.dma_start(xb[u][:, :], x2_t[i * U + u]).then_inc(sem(f"xb_in{u}"), 16)
            sp.wait_ge(sem("disp_done"), 2 * NT)
            with sp.Fori(0, NQ // 2) as i:
                for u in range(2):
                    sp.wait_ge(sem(f"ffn2_full{u}"), i + 1)
                    sp.dma_start(f1q[u][:, :, :], f1[:, :, bass.ts(i * 2 + u, P)]).then_inc(sem(f"fq_in{u}"), 16)
                    sp.dma_start(f2q[u][:, :], f2[i * 2 + u]).then_inc(sem(f"fq_in{u}"), 16)
            sp.wait_ge(sem("ffn_done"), 2 * NQ)
            with sp.Fori(0, NT // 2) as i:
                for u in range(2):
                    sp.wait_ge(sem(f"sum3_{u}"), i + 1)
                    sp.dma_start(xc[u][:, :], x2_t[i * 2 + u]).then_inc(sem(f"xc_in{u}"), 16)

        @block.tensor
        def _(pe):
            def mm(o, l, r, start=True, stop=True):
                return nc.tensor.matmul(o, l, r, start=start, stop=stop, skip_group_check=True)

            def mm3(o, lh, ll, rh, rl, first, last):
                mm(o, lh, rh, start=first, stop=False)
                mm(o, lh, rl, start=False, stop=False)
                return mm(o, ll, rh, start=False, stop=last)

            prime(pe, "disp_pe", "ffn2_full0", "ffn2_full1", "inter_pe0", "inter_pe1", "comb_pe0", "comb_pe1")
            pe.wait_ge(sem("small_in"), 16 * 7)
            for r in range(8):
                if r:
                    pe.wait_ge(sem("pow_evac"), r)
                src, n = (pw, 1 << r) if r < 4 else (qw, 1 << (r - 4))
                m = 7 if r == 7 else n
                mm(scp[r % 2][0:SD, 0:m * SD], tpw[r][:, :], src[:, 1:1 + m, :].rearrange("p a b -> p (a b)"))
                last = mm(scp[r % 2][0:SD, 512:512 + SD], src[:, n, :], tpw[r][:, :])
                last.then_inc(sem("pow_pe"), 1)
            pe.wait_ge(sem("pow_evac"), 4)
            for n in range(4):
                k, hf = n // 2, n % 2
                if n >= 2:
                    pe.wait_ge(sem("ba_evac"), n - 1)
                mm(sp_[n % 2][:, :], bmt[:, k * P:(k + 1) * P],
                   pw[:, 8 * hf:8 * hf + 8, :].rearrange("p a b -> p (a b)")).then_inc(sem("ba_pe"), 1)
            pe.wait_ge(sem("ba_evac"), 4)
            pe.wait_ge(sem("xTa_in"), 16 * 5)
            for i in range(RAD):
                for k in range(KT):
                    last = mm(pp[0][0:SD, 0:B * RAD], ba[:, k, RAD - 1 - i, :],
                              xTa[:, k, :].rearrange("p (n i) -> p i n", i=RAD)[:, i, :],
                              start=(i == 0 and k == 0), stop=(i == RAD - 1 and k == KT - 1))
            last.then_inc(sem("pre_pe"), 1)
            for g in range(NT):
                if g % 8 == 0 and g >= 16:
                    pe.wait_ge(sem("router_evac"), g // 8 - 1)
                for k in range(KT):
                    last = mm(sp_[g // 8 % 2][:, (g % 8) * NC:(g % 8 + 1) * NC], xTa[:, k, g * P:(g + 1) * P],
                              wrt[:, k, :], start=(k == 0), stop=(k == KT - 1))
                if g % 8 == 7:
                    last.then_inc(sem("router_pe"), 1)
            pe.wait_ge(sem("pre_dve"), PRE_DVE["scan1_evac"])
            pe.wait_ge(sem("pow_evac"), 8)
            for j in range(RAD):
                last = mm(pp[1][0:SD, 0:B], qw[:, RAD - 1 - j, :], gt[:, :, j], start=(j == 0), stop=(j == RAD - 1))
            last.then_inc(sem("pre_pe"), 1)
            pe.wait_ge(sem("pre_dve"), PRE_DVE["scan2_evac"])
            for k in range(KT):
                last = mm(pp[1][:, 32 + k * B:32 + (k + 1) * B], wit[:, k * P:(k + 1) * P], ht[:, :])
            last.then_inc(sem("pre_pe"), 1)
            pe.wait_ge(sem("pre_dve"), PRE_DVE["hm_evac"])
            for b in range(B):
                for k in range(KT):
                    last = mm(pp[0][0:B, 0:S], hm[:, k, b, :], xTa[:, k, b * S:(b + 1) * S],
                              start=(b == 0 and k == 0), stop=(b == B - 1 and k == KT - 1))
            last.then_inc(sem("pre_pe"), 1)
            pe.wait_ge(sem("pre_dve"), PRE_DVE["imp_sm"])
            for t in range(TT):
                last = nc.tensor.transpose(pp[1][:, t * B:(t + 1) * B], impe[:, t * P:(t + 1) * P], idn[0:B, 0:B])
            last.then_inc(sem("pre_pe"), 1)
            pe.wait_ge(sem("pre_dve"), PRE_DVE["uw_done"])
            for b in range(B):
                for t in range(TT):
                    g = b * TT + t
                    last = mm(pp[0][0:NC, b:b + 1], rte[:, g, :], uw[:, g:g + 1], start=(t == 0), stop=(t == TT - 1))
            last.then_inc(sem("pre_pe"), 1)
            pe.wait_ge(sem("pre_dve"), PRE_DVE["nw_evac"])
            mm(pp[1][0:NC, 0:B], ones[:, :], nw[:, 0, :]).then_inc(sem("pre_pe"), 1)
            pe.wait_ge(sem("pre_dve"), PRE_DVE["nd_done"])
            for n in range(32):
                if n % 2 == 0:
                    pe.wait_ge(sem(f"comp_in{n // 2 % 2}"), 16 * (n // 4 + 1))
                if n >= 2:
                    pe.wait_ge(sem("sc_evac"), n - 1)
                mm(sp_[n % 2][0:B * KT, :], nd[:, :, :].rearrange("p b k -> p (b k)"),
                   cst[n // 2 % 2][:, (n % 2) * 512:(n % 2 + 1) * 512]).then_inc(sem("comp_used"), 1)
            pe.wait_ge(sem("sc_evac"), 32)
            pe.wait_ge(sem("stage_split"), len(STAGES))
            pe.wait_ge(sem("stage_hi"), len(STAGES))
            pe.wait_ge(sem("main_const"), 16 * 4)
            pe.wait_ge(sem("qz_zero"), 1)

            def scores(t, h):
                tile, ch = h // NCH, h % NCH
                t.w(pe, "cand_done", H, h - 1, t.a)
                for n in range(CH // 512):
                    kc = slice(ch * CH + n * 512, ch * CH + (n + 1) * 512)
                    tc = slice(tile * P, (tile + 1) * P)
                    last = mm3(scp[h % 2][:, n * 512:(n + 1) * 512], qth[:, tc], qtl[:, tc], kh[:, kc], kl[:, kc],
                               True, True)
                last.then_inc(sem("score_full"), 1)

            def pv(t, p):
                j = J_PV + p
                t.w(pe, "clip_done", H, 2 * p + 2, t.c)
                job_free(pe, t, j)
                bank = pp[j % 2]
                for k in range(KT):
                    for o in range(2):
                        h = 2 * p + o
                        mm(bank[64 * o:64 * o + 64, 0:S], vv[:, k, h * DH:(h + 1) * DH], ex[h % 4][:, k, :],
                           start=(k == 0), stop=(k == KT - 1))
                for k in range(KT):
                    for o in range(2):
                        last = mm(bank[64 * o:64 * o + 64, S:2 * S], mb[:, k, :], ex[(2 * p + o) % 4][:, k, :],
                                  start=(k == 0), stop=(k == KT - 1))
                last.then_inc(sem(f"proj_full{j % 2}"), 1)

            def body(t):
                if t.attn:
                    t.w(pe, "x_lo", 1, 1, t.a)
                    t.w(pe, "sc_lo", 1, 1, t.a)
                    t.w(pe, "exp_done", H, 0, t.c)
                    for k in range(KT):
                        last = mm3(sp_[0][:, 0:S], sch[:, k, :], scl[:, k, :], xth[:, k, :], xtl[:, k, :],
                                   k == 0, k == KT - 1)
                    last.then_inc(sem("q_full"), 1)
                if t.cross:
                    t.w(pe, "cm_lo", 1, 1, t.c)
                    for m in range(4):
                        j = J_K + m
                        job_free(pe, t, j)
                        for o in range(2):
                            cs = slice((2 * m + o) * P, (2 * m + o + 1) * P)
                            for k in range(KT):
                                last = mm3(pp[j % 2][:, o * S:(o + 1) * S], wh[:, 1, k, cs], wl[:, 1, k, cs],
                                           cmh[:, k, :], cml[:, k, :], k == 0, k == KT - 1)
                        last.then_inc(sem(f"proj_full{j % 2}"), 1)
                    t.w(pe, "ctx_lo", 1, 1, t.c)
                    for m in range(4):
                        j, tile, hf = J_V + m, m // 2, m % 2
                        job_free(pe, t, j)
                        for k in range(KT):
                            tc, cs = slice(tile * P, (tile + 1) * P), slice(hf * 512, (hf + 1) * 512)
                            last = mm3(pp[j % 2][:, :], cth[:, k, tc], ctl[:, k, tc], wh[:, 2, k, cs], wl[:, 2, k, cs],
                                       k == 0, k == KT - 1)
                        last.then_inc(sem(f"proj_full{j % 2}"), 1)
                    for tile in range(TT):
                        j = J_X1 + tile
                        t.w(pe, "x1_done", TT, tile + 1, t.c)
                        job_free(pe, t, j)
                        for k in range(KT):
                            last = nc.tensor.transpose(pp[j % 2][:, k * P:(k + 1) * P], x1[:, tile, k * P:(k + 1) * P],
                                                       idn[:, :])
                        last.then_inc(sem(f"proj_full{j % 2}"), 1)
                    for m in range(4):
                        j = J_Q + m
                        job_free(pe, t, j)
                        if m == 0:
                            job_done(pe, t, J_X1)
                            job_done(pe, t, J_X1 + 1)
                        for o in range(2):
                            cs = slice((2 * m + o) * P, (2 * m + o + 1) * P)
                            for k in range(KT):
                                last = mm3(pp[j % 2][:, o * S:(o + 1) * S], wh[:, 0, k, cs], wl[:, 0, k, cs],
                                           x1h[:, k, :], x1l[:, k, :], k == 0, k == KT - 1)
                        last.then_inc(sem(f"proj_full{j % 2}"), 1)
                if t.attn:
                    t.w(pe, "q_lo", 1, 1, t.a)
                for h in range(H):
                    if t.attn:
                        scores(t, h)
                    if t.cross:
                        if h == 0:
                            job_done(pe, t, J_Q + 2)
                            job_done(pe, t, J_Q + 3)
                            t.w(pe, "mb_done", 1, 1, t.c)
                        t.w(pe, "exp_done", H, max(h - 1, 0), t.c)
                        for k in range(KT):
                            last = mm(sp_[h % 2][:, k * S:(k + 1) * S], kt[:, h // 2, k * P:(k + 1) * P], qz[:, h, :])
                        last.then_inc(sem("sim_full"), 1)
                        if h % 2 and h >= 3:
                            pv(t, (h - 3) // 2)
                if t.cross:
                    pv(t, NP - 1)
                    for tile in range(TT):
                        j = J_WO + tile
                        job_free(pe, t, j)
                        if tile == 0:
                            job_done(pe, t, J_PV + NP - 2)
                            job_done(pe, t, J_PV + NP - 1)
                        for p in range(NP):
                            last = mm(pp[j % 2][:, 0:D], ot[:, p, tile * P:(tile + 1) * P], wo[:, p, :],
                                      start=(p == 0), stop=(p == NP - 1))
                        last.then_inc(sem(f"proj_full{j % 2}"), 1)

            turns(pe, body)

            e_small = [sp_[0], sp_[1], pp[0], pp[1]]
            e_disp = [scp[0][:, 0:512], scp[0][:, 512:1024], scp[1][:, 0:512], scp[1][:, 512:1024]]
            pe.wait_ge(sem("e_const"), 16 * 3)
            pe.wait_ge(sem("bd_zero"), 1)
            with pe.Fori(0, NT // U) as i:
                for u in range(U):
                    pe.wait_ge(sem(f"xb_in{u}"), i * 16 + 16)
                    pe.wait_ge(sem("bd_done"), i * U + 1)
                    for k in range(KT):
                        last = nc.tensor.transpose(e_small[u][:, k * P:(k + 1) * P], xb[u][:, k * P:(k + 1) * P],
                                                   idn[:, :])
                    last.then_inc(sem("xbT_pe"), 1)
                for u in range(U):
                    pe.wait_ge(sem("xbT_evac"), i * U + u + 1)
                    for k in range(KT):
                        last = mm(e_small[u][:, 256:384], ctr[:, k, :], xbt[u][:, k, :], start=(k == 0),
                                  stop=(k == KT - 1))
                    last.then_inc(sem("logit_pe"), 1)
                for u in range(U):
                    pe.wait_ge(sem("perm_done"), i * U + u + 1)
                    nc.tensor.transpose(e_small[u][:, 384:512], pm[u][:, :, :].rearrange("p g t -> p (g t)"),
                                        idn[:, :]).then_inc(sem("perm_pe"), 1)
                for u in range(U):
                    pe.wait_ge(sem("bd_done"), i * U + u + 2)
                    if u >= 2:
                        pe.wait_ge(sem(f"disp_act{u % 2}"), i * 2 + 2)
                        pe.wait_ge(sem(f"disp_dve{u % 2}"), i * 2 + 2)
                    else:
                        pe.wait_ge(sem(f"disp_act{u % 2}"), i * 2 + 1)
                        pe.wait_ge(sem(f"disp_dve{u % 2}"), i * 2 + 1)
                    for k in range(KT):
                        last = mm(e_disp[2 * (u % 2) + k], xb[u][:, k * P:(k + 1) * P],
                                  bd[u][:, :, :].rearrange("p g s -> p (g s)"))
                    last.then_inc(sem("disp_pe"), 1)
            pe.wait_ge(sem("hb_zero"), 1)
            pe.wait_ge(sem("disp_done"), 2 * NT)
            with pe.Fori(0, NQ // 2) as i:
                for u in range(2):
                    pe.wait_ge(sem(f"fq_in{u}"), i * 32 + 32)
                    pe.wait_ge(sem(f"hidden_done{u}"), i + 1)
                    for k in range(KT):
                        rhs = dtt[:, k, :, :].rearrange("p s g -> p (s g)")[:, bass.ts(i * 2 + u, 512)]
                        last = mm(sp_[u][:, :], f1q[u][:, k, :], rhs, start=(k == 0), stop=(k == KT - 1))
                    last.then_inc(sem(f"ffn1_full{u}"), 1)
                for u in range(2):
                    pe.wait_ge(sem(f"hidden_done{u}"), i + 2)
                    pe.wait_ge(sem(f"ffn2_act{u}"), i + 1)
                    pe.wait_ge(sem(f"ffn2_dve{u}"), i + 1)
                    for k in range(KT):
                        last = mm(e_disp[2 * u + k], f2q[u][:, k * P:(k + 1) * P],
                                  hb[u][:, :, :].rearrange("p s g -> p (s g)"))
                    last.then_inc(sem(f"ffn2_full{u}"), 1)
            with pe.Fori(0, NT // 2) as i:
                for u in range(2):
                    pe.wait_ge(sem(f"gi_act{u}"), i + 1)
                    pe.wait_ge(sem(f"gi_dve{u}"), i + 1)
                    pe.wait_ge(sem(f"inter_act{u}"), i + 1)
                    pe.wait_ge(sem(f"inter_dve{u}"), i + 1)
                    for g in range(4):
                        for k in range(KT):
                            last = nc.tensor.transpose(e_disp[2 * u + g // 2][:, (g % 2) * D + k * P:(g % 2) * D + (k + 1) * P],
                                                       gi[u][:, k, g, :], idn[:, :])
                    last.then_inc(sem(f"inter_pe{u}"), 1)
                for u in range(2):
                    pe.wait_ge(sem(f"inter_act{u}"), i + 2)
                    pe.wait_ge(sem(f"inter_dve{u}"), i + 2)
                    pe.wait_ge(sem(f"pms_done{u}"), i + 1)
                    pe.wait_ge(sem(f"sum3_{u}"), i + 1)
                    for g in range(4):
                        last = mm(pp[u][GT * g:GT * (g + 1), 0:D], pms[u][:, GT * g:GT * (g + 1)], it_[u][:, g, :])
                    last.then_inc(sem(f"comb_pe{u}"), 1)

        @block.scalar
        def _(act):
            prime(act, "proj_free0", "proj_free1", "exp_done", "bd_done", "disp_act0", "disp_act1", "hidden_done0",
                  "hidden_done1", "ffn2_act0", "ffn2_act1", "inter_act0", "inter_act1", "pma_done")
            for n, (src, c, hi, lo) in enumerate(STAGES):
                if n >= 2:
                    act.wait_ge(sem("stage_split"), n - 1)
                    act.wait_ge(sem("stage_hi"), n - 1)
                act.dma_start(stg[n % 2][:, :], src[:, c * STW:(c + 1) * STW]).then_inc(sem(f"stage_in{n % 2}"), 16)
                if n >= 1:
                    m = n - 1
                    act.wait_ge(sem(f"stage_in{m % 2}"), 16 * (m // 2 + 1))
                    nc.scalar.copy(STAGES[m][2], stg[m % 2][:, :]).then_inc(sem("stage_hi"), 1)
            m = len(STAGES) - 1
            act.wait_ge(sem(f"stage_in{m % 2}"), 16 * (m // 2 + 1))
            nc.scalar.copy(STAGES[m][2], stg[m % 2][:, :]).then_inc(sem("stage_hi"), 1)
            for dst, src in ((wo[:, :, :], Wo), (bob[:, :], bo), (cix[:, :, :], cidx), (mcu[:, :, :], mcol)):
                act.dma_start(dst, src).then_inc(sem("main_const"), 16)
            for n in range(4):
                act.wait_ge(sem("router_sub"), n + 1)
                nc.scalar.activation(rte[:, 8 * n:8 * n + 8, :], rte[:, 8 * n:8 * n + 8, :], ACT.Exp)\
                    .then_inc(sem("router_exp"), 1)
            act.wait_ge(sem("pre_dve"), PRE_DVE["imp_max"])
            nc.scalar.activation(impe[:, :], pp[0][0:B, 0:S], ACT.Exp, bias=imx[:, 0:1], accum_out=imx[:, 1:2])\
                .then_inc(sem("imp_exp"), 1)
            for n in range(32):
                act.wait_ge(sem("comp_used"), n + 1)
                if n >= 2:
                    act.wait_ge(sem(f"sc_store{n % 2}"), 16 * (n // 2))
                nc.scalar.copy(scs[n % 2], sp_[n % 2][0:B * KT, :]).then_inc(sem("sc_evac"), 1)
            act.wait_ge(sem("stage_split"), len(STAGES))
            act.wait_ge(sem("sc_store0"), 256)
            act.wait_ge(sem("sc_store1"), 256)

            def weights8(t, tile, batch):
                t.w(act, "idx_done", TT, tile + 1, batch)
                nc.scalar.activation(w8[:, tile, :], v8[:, tile, :], ACT.Exp, bias=nb[:, tile:tile + 1], scale=K_SCALE,
                                     accum_out=wsum[:, tile, 0:1]).then_inc(sem("w8_exp"), 1)

            def body(t):
                if t.attn:
                    t.w(act, "xt_in", 16, 16, t.a)
                    t.w(act, "q_full", 1, 0, t.a)
                    nc.scalar.copy(xth[:, :, :], xt[:, :, :]).then_inc(sem("x_hi"), 1)
                    t.w(act, "sct_in", 16, 16, t.a)
                    nc.scalar.copy(sch[:, :, :], sct[:, :, :]).then_inc(sem("sc_hi"), 1)
                    t.w(act, "q_full", 1, 1, t.a)
                    nc.scalar.copy(qth[:, :], sp_[0][:, 0:S]).then_inc(sem("q_hi"), 1)
                if t.cross:
                    weights8(t, 1, t.c)
                    t.w(act, "cm_done", 1, 1, t.c)
                    nc.scalar.copy(cmh[:, :, :], cm[:, :, :]).then_inc(sem("cm_hi"), 1)
                    nc.scalar.copy(cth[:, :, :], ct[:, :, :]).then_inc(sem("ctx_hi"), 1)
                    for m in range(4):
                        job_full(act, t, J_K + m)
                        nc.scalar.copy(kt[:, 2 * m:2 * m + 2, :].rearrange("p a s -> p (a s)"), pp[m % 2][:, :])\
                            .then_inc(sem(f"proj_free{m % 2}"), 1)
                    for m in range(4):
                        job_full(act, t, J_V + m)
                        if m == 0:
                            t.w(act, "mb_done", 1, 1, t.c)
                        nc.scalar.mul(vv[:, m // 2, 512 * (m % 2):512 * (m % 2) + 512], pp[m % 2][:, :],
                                      mb[:, m // 2, 0:1]).then_inc(sem(f"proj_free{m % 2}"), 1)
                    for tile in range(TT):
                        j = J_X1 + tile
                        job_full(act, t, j)
                        nc.scalar.copy(x1h[:, :, tile * P:(tile + 1) * P],
                                       pp[j % 2][:, 0:D].rearrange("p (k s) -> p k s", k=KT)).then_inc(sem("x1_hi"), 1)
                    for m in range(4):
                        j = J_Q + m
                        job_full(act, t, j)
                        for o in range(2):
                            r = slice(64 * o, 64 * o + 64)
                            last = nc.scalar.copy(
                                qz[r, 4 * m:4 * m + 4, :].rearrange("p (a o) s -> p a o s", o=2)[:, :, o, :],
                                pp[j % 2][r, :].rearrange("p (a s) -> p a s", a=2))
                        last.then_inc(sem(f"proj_free{j % 2}"), 1)
                for h in range(H):
                    if t.cross:
                        t.w(act, "sim_full", H, h + 1, t.c)
                        p = (h - 4) // 2
                        if p >= 0:
                            job_full(act, t, J_PV + p)
                        nc.scalar.activation(ex[h % 4][:, :, :].rearrange("p k s -> p (k s)"), sp_[h % 2][:, :],
                                             ACT.Exp, scale=A_SCALE).then_inc(sem("exp_done"), 1)
                    if t.attn and h == 10:
                        weights8(t, 0, t.a)

            turns(act, body)

            act.wait_ge(sem("x2_stored"), 16 * B)
            e_small = [sp_[0], sp_[1], pp[0], pp[1]]
            e_disp = [scp[0][:, 0:512], scp[0][:, 512:1024], scp[1][:, 0:512], scp[1][:, 512:1024]]
            with act.Fori(0, NT // U) as i:
                for u in range(U):
                    act.wait_ge(sem("xbT_pe"), i * U + u + 1)
                    nc.scalar.copy(xbt[u][:, :, :].rearrange("p k s -> p (k s)"), e_small[u][:, 0:256])\
                        .then_inc(sem("xbT_evac"), 1)
                for u in range(U):
                    act.wait_ge(sem("perm_done"), i * U + u + 1)
                    nc.scalar.copy(pma[:, bass.ts(i * U + u, P)], pm[u][:, :, :].rearrange("p g t -> p (g t)"))\
                        .then_inc(sem("pma_done"), 1)
                    act.wait_ge(sem("perm_pe"), i * U + u + 1)
                    act.wait_ge(sem("disp_pe"), i * U + 1)
                    for g in range(4):
                        r = slice(GT * g, GT * (g + 1))
                        last = nc.scalar.copy(bd[u][r, g, :], e_small[u][r, 384:512])
                    last.then_inc(sem("bd_done"), 1)
                for u in range(U):
                    act.wait_ge(sem("disp_pe"), i * U + u + 2)
                    dst = dtt[:, 0, :, bass.ts(i * U + u, 4)].rearrange("p s g -> p g s")
                    nc.scalar.copy(dst, e_disp[2 * (u % 2)].rearrange("p (g s) -> p g s", g=4))\
                        .then_inc(sem(f"disp_act{u % 2}"), 1)
            act.wait_ge(sem("hb_zero"), 1)
            with act.Fori(0, NQ // 2) as i:
                for u in range(2):
                    act.wait_ge(sem(f"ffn1_full{u}"), i + 1)
                    act.wait_ge(sem(f"ffn2_full{u}"), i + 1)
                    act.wait_ge(sem(f"fbs_done{u}"), i + 1)
                    for s in range(4):
                        r = slice(F * s, F * (s + 1))
                        last = nc.scalar.activation(hb[u][r, s, :], sp_[u][r, s * NG:(s + 1) * NG], ACT.Relu,
                                                    bias=zz[u][r, 0:1])
                    last.then_inc(sem(f"hidden_done{u}"), 1)
                for u in range(2):
                    act.wait_ge(sem(f"ffn2_full{u}"), i + 2)
                    dst = dtt[:, 0, :, :].rearrange("p s g -> p (s g)")[:, bass.ts(i * 2 + u, 512)]
                    nc.scalar.copy(dst, e_disp[2 * u]).then_inc(sem(f"ffn2_act{u}"), 1)
            act.wait_ge(sem("ffn_done"), 2 * NQ)
            with act.Fori(0, NT // 2) as i:
                for u in range(2):
                    act.wait_ge(sem(f"inter_pe{u}"), i + 1)
                    src = dtt[:, 0, :, bass.ts(i * 2 + u, 4)].rearrange("p s g -> p g s")
                    nc.scalar.copy(gi[u][:, 0, :, :], src).then_inc(sem(f"gi_act{u}"), 1)
                    act.wait_ge(sem(f"comb_pe{u}"), i + 1)
                    nc.scalar.copy(pms[u][:, :], pma[:, bass.ts(i * 2 + u, P)]).then_inc(sem(f"pms_done{u}"), 1)
                for u in range(2):
                    act.wait_ge(sem(f"inter_pe{u}"), i + 2)
                    nc.scalar.copy(it_[u][:, 0:2, :].rearrange("p g d -> p (g d)"), e_disp[2 * u])\
                        .then_inc(sem(f"inter_act{u}"), 1)

        @block.vector
        def _(dve):
            def after(name, ins, n):
                ins.then_inc(sem(name), 1)
                dve.wait_ge(sem(name), n)

            prime(dve, "sum3_0", "sum3_1", "disp_dve0", "disp_dve1", "ffn2_dve0", "ffn2_dve1", "inter_dve0", "inter_dve1")
            nc.vector.memset(neghalf[:, :], -0.5).then_inc(sem("v_const"), 1)
            nc.vector.memset(ones[:, :], 1.0).then_inc(sem("v_const"), 1)
            after("v_const", nc.vector.memset(hm[:, :, :, :], 0.0), 3)
            after("v_const", nc.vector.memset(nd[:, :, :], 0.0), 4)
            for r in range(8):
                dve.wait_ge(sem("pow_pe"), r + 1)
                dst, n = (pw, 1 << r) if r < 4 else (qw, 1 << (r - 4))
                m = 7 if r == 7 else n
                last = nc.vector.tensor_copy(dst[:, n + 1:n + 1 + m, :].rearrange("p a b -> p (a b)"),
                                             scp[r % 2][0:SD, 0:m * SD])
                if r < 7:
                    last = nc.vector.tensor_copy(tpw[r + 1][:, :], scp[r % 2][0:SD, 512:512 + SD])
                if r == 3:
                    last = nc.vector.tensor_copy(qw[:, 1, :], scp[r % 2][0:SD, 7 * SD:8 * SD])
                last.then_inc(sem("pow_evac"), 1)
            for n in range(4):
                dve.wait_ge(sem("ba_pe"), n + 1)
                nc.vector.tensor_copy(ba[:, n // 2, 8 * (n % 2):8 * (n % 2) + 8, :].rearrange("p a b -> p (a b)"),
                                      sp_[n % 2][:, :]).then_inc(sem("ba_evac"), 1)
            dve.wait_ge(sem("pre_pe"), PRE_PE["scan1"])
            nc.vector.tensor_copy(gt[:, :, :].rearrange("p b j -> p (b j)"), pp[0][0:SD, 0:B * RAD])\
                .then_inc(sem("pre_dve"), 1)
            for n in range(4):
                dve.wait_ge(sem("router_pe"), n + 1)
                src = sp_[n % 2][:, :].rearrange("p (g n) -> p g n", n=NC)
                after("router_max", nc.vector.tensor_reduce(rmx[:, 8 * n:8 * n + 8], src, AX, ALU.max), n + 1)
                nc.vector.tensor_tensor(rte[:, 8 * n:8 * n + 8, :], src,
                                        rmx[:, 8 * n:8 * n + 8].unsqueeze(2).to_broadcast([P, 8, NC]),
                                        ALU.subtract).then_inc(sem("router_sub"), 1)
                dve.wait_ge(sem("router_sub"), n + 1)
                nc.vector.tensor_copy(uw[:, 8 * n:8 * n + 8], rmx[:, 8 * n:8 * n + 8]).then_inc(sem("router_evac"), 1)
            dve.wait_ge(sem("pre_pe"), PRE_PE["scan2"])
            nc.vector.tensor_copy(ht[:, :], pp[1][0:SD, 0:B]).then_inc(sem("pre_dve"), 1)
            dve.wait_ge(sem("pre_pe"), PRE_PE["hproj"])
            for k in range(KT):
                last = nc.vector.tensor_copy(hm[:, k, :, :].rearrange("p a b -> p (a b)")[:, 0:B * B:B + 1],
                                             pp[1][:, 32 + k * B:32 + (k + 1) * B])
            last.then_inc(sem("pre_dve"), 1)
            for n in range(4):
                dve.wait_ge(sem("router_exp"), n + 1)
                nc.vector.tensor_reduce(rsm[:, 8 * n:8 * n + 8], rte[:, 8 * n:8 * n + 8, :], AX, ALU.add)\
                    .then_inc(sem("router_sum"), 1)
            dve.wait_ge(sem("router_sum"), 4)
            dve.wait_ge(sem("router_evac"), 4)
            after("router_rec", nc.vector.reciprocal(uw[:, :], rsm[:, :]), 1)
            dve.wait_ge(sem("pre_pe"), PRE_PE["imp_pe"])
            nc.vector.tensor_reduce(imx[:, 0:1], pp[0][0:B, 0:S], AX, ALU.max, negate=True)\
                .then_inc(sem("pre_dve"), 1)
            dve.wait_ge(sem("imp_exp"), 1)
            after("imp_rec", nc.vector.reciprocal(imx[:, 2:3], imx[:, 1:2]), 1)
            nc.vector.tensor_scalar(impe[:, :], impe[:, :], imx[:, 2:3], None, ALU.mult).then_inc(sem("pre_dve"), 1)
            dve.wait_ge(sem("pre_pe"), PRE_PE["impT_pe"])
            nc.vector.tensor_tensor(uw[:, :].rearrange("p (b t) -> p t b", t=TT), uw[:, :].rearrange("p (b t) -> p t b", t=TT),
                                    pp[1][:, 0:TT * B].rearrange("p (t b) -> p t b", t=TT), ALU.mult)\
                .then_inc(sem("pre_dve"), 1)
            dve.wait_ge(sem("pre_pe"), PRE_PE["nw_pe"])
            nc.vector.tensor_copy(nw[:, 0, :], pp[0][0:NC, 0:B]).then_inc(sem("pre_dve"), 1)
            dve.wait_ge(sem("pre_pe"), PRE_PE["nws_pe"])
            after("nw_chain", nc.vector.tensor_scalar(nw[:, 1, :], pp[1][0:NC, 0:B], 1e-8, None, ALU.add), 1)
            after("nw_chain", nc.vector.reciprocal(nw[:, 2, :], nw[:, 1, :]), 2)
            for k in range(KT):
                last = nc.vector.tensor_tensor(nd[k * NC:(k + 1) * NC, :, k], nw[:, 0, :], nw[:, 2, :], ALU.mult)
            last.then_inc(sem("pre_dve"), 1)
            dve.wait_ge(sem("stage_split"), len(STAGES))
            dve.wait_ge(sem("sc_store0"), 256)
            dve.wait_ge(sem("sc_store1"), 256)
            dve.wait_ge(sem("main_const"), 16 * 4)
            after("mv_done", nc.vector.tensor_scalar(mv[:, :, :], mcu[:, :, :], E_LO, None, ALU.max), 1)
            nc.vector.memset(qz[:, :, :], 0.0).then_inc(sem("qz_zero"), 1)

            CHAIN = {"links": 0}

            def body(t):
                n = [0]

                def own(ins, solo=False):
                    n[0] += 1
                    ins.then_inc(sem("own"), 1)
                    if isinstance(t.c, int):
                        base = 0 if t.c < 0 else OWN_A + (B - 1) * OWN_F
                    else:
                        base = t.c * OWN_F + OWN_A
                    if solo:
                        wait_apart(dve, "own", base + n[0])
                    else:
                        dve.wait_ge(sem("own"), base + n[0])

                def merge(tile):
                    own(nc.vector.max(v8[:, tile, :], cv[:, tile, :]), solo=True)
                    own(nc.vector.max_index(p8[:, :], v8[:, tile, :], cv[:, tile, :]))
                    own(nc.vector.tensor_tensor(cf[:, :], ci[:, tile, :], cix[:, 0, :], ALU.add))
                    own(nc.vector.tensor_tensor(eq, cix[:, 1, :].unsqueeze(1).to_broadcast([P, TOPK, NCH * 8]),
                                                p8[:, :].unsqueeze(2).to_broadcast([P, TOPK, NCH * 8]), ALU.is_equal))
                    own(nc.vector.tensor_tensor(eq, eq,
                                                cf[:, :].unsqueeze(1).to_broadcast([P, TOPK, NCH * 8]), ALU.mult))
                    nc.vector.tensor_scalar(nb[:, tile:tile + 1], v8[:, tile, 0:1], -K_SCALE, None, ALU.mult)
                    with nc.allow_low_precision(reason="one index below 2^24 and zeros: exact"):
                        nc.vector.tensor_reduce(i8[:, tile, :], eq, AX, ALU.add).then_inc(sem("idx_done"), 1)
                    t.w(dve, "idx_done", TT, tile + 1, t.a)

                def value_sum(tile, batch):
                    t.w(dve, "w8_exp", TT, tile + 1, batch)
                    own(nc.vector.reciprocal(wsum[:, tile, 1:2], wsum[:, tile, 0:1]))
                    own(nc.vector.tensor_scalar(w8[:, tile, :], w8[:, tile, :], wsum[:, tile, 1:2], None, ALU.mult))
                    t.w(dve, "xn_in", 16, 16, batch)
                    t.w(dve, "vg_in", 16 * TOPK * TT, 16 * TOPK * (tile + 1), batch)
                    for k in range(TOPK):
                        prev = xn[:, tile, :] if k == 0 else acc
                        own(nc.vector.scalar_tensor_tensor(acc, vg[:, k, :], w8[:, tile, k:k + 1], prev,
                                                           ALU.mult, ALU.add))
                    own(nc.vector.bn_stats(st[:, 0:6], acc), solo=True)
                    own(nc.vector.bn_aggr(ag[:, 0:2], st[:, 0:6]))
                    nc.vector.tensor_scalar(ve[:, 0:1], ag[:, 1:2], EPS, None, ALU.add).then_inc(sem("sum_done"), 1)

                def value_norm(tile, batch):
                    t.w(dve, "rstd1", TT, tile + 1, batch)
                    nc.vector.tensor_scalar(x1[:, tile, :], acc, ag[:, 0:1], rs[:, 0:1], ALU.subtract, ALU.mult)\
                        .then_inc(sem("x1_done"), 1)

                def norm(p):
                    j = J_PV + p
                    if p:
                        job_done(dve, t, j - 1)
                    job_full(dve, t, j)
                    own(nc.vector.reciprocal(rd, pp[j % 2][:, S:2 * S]))
                    nc.vector.tensor_tensor(ot[:, p, :], pp[j % 2][:, 0:S], rd, ALU.mult)\
                        .then_inc(sem(f"proj_free{j % 2}"), 1)

                if t.attn:
                    t.w(dve, "x_hi", 1, 1, t.a)
                    nc.vector.tensor_tensor(xtl[:, :, :], xt[:, :, :], xth[:, :, :].bitcast(F32), ALU.subtract)\
                        .then_inc(sem("x_lo"), 1)
                    t.w(dve, "sc_hi", 1, 1, t.a)
                    nc.vector.tensor_tensor(scl[:, :, :], sct[:, :, :], sch[:, :, :].bitcast(F32), ALU.subtract)\
                        .then_inc(sem("sc_lo"), 1)
                    t.w(dve, "q_hi", 1, 1, t.a)
                    nc.vector.tensor_tensor(qtl[:, :], sp_[0][:, 0:S], qth[:, :].bitcast(F32), ALU.subtract)\
                        .then_inc(sem("q_lo"), 1)
                if t.cross:
                    t.w(dve, "ct_in", 16, 16, t.c)
                    t.w(dve, "mr_in", 16, 16, t.c)
                    t.w(dve, "cm_lo", 1, 0, t.c)
                    nc.vector.tensor_tensor(cm[:, :, :], ct[:, :, :], mr[:, :].unsqueeze(1).to_broadcast([P, KT, S]),
                                            ALU.mult).then_inc(sem("cm_done"), 1)
                    nc.vector.tensor_copy(mb[:, :, :], mv[:, :, bass.ts(t.c, 1)].to_broadcast([P, KT, DH]))\
                        .then_inc(sem("mb_done"), 1)
                    value_sum(1, t.c)
                    value_norm(1, t.c)
                    for tile in range(TT):
                        j = J_X1 + tile
                        t.w(dve, "x1_hi", TT, tile + 1, t.c)
                        nc.vector.tensor_tensor(x1l[:, :, tile * P:(tile + 1) * P],
                                                pp[j % 2][:, 0:D].rearrange("p (k s) -> p k s", k=KT),
                                                x1h[:, :, tile * P:(tile + 1) * P].bitcast(F32), ALU.subtract)\
                            .then_inc(sem(f"proj_free{j % 2}"), 1)
                for h in range(H):
                    if t.attn:
                        tile, ch = h // NCH, h % NCH
                        t.w(dve, "score_full", H, h + 1, t.a, apart=True)
                        own(nc.vector.max(cv[:, tile, ch * 8:ch * 8 + 8], scp[h % 2][:, :]), solo=True)
                        nc.vector.max_index(ci[:, tile, ch * 8:ch * 8 + 8], cv[:, tile, ch * 8:ch * 8 + 8],
                                            scp[h % 2][:, :]).then_inc(sem("cand_done"), 1)
                    if t.cross and h % 2 and h >= 3:
                        norm((h - 3) // 2)
                    if t.attn and h == 8:
                        t.w(dve, "cand_done", H, 9, t.a, apart=True)
                        merge(0)
                    if t.attn and h == 12:
                        value_sum(0, t.a)
                    if t.attn and h == 13:
                        value_norm(0, t.a)
                if t.attn:
                    t.w(dve, "cand_done", H, 16, t.a, apart=True)
                    merge(1)
                if t.cross:
                    norm(NP - 1)
                    t.w(dve, "x1r_done", 1, 1, t.c)
                    for tile in range(TT):
                        j = J_WO + tile
                        job_full(dve, t, j)
                        ins = nc.vector.tensor_tensor(z2[:, tile, :], pp[j % 2][:, 0:D], x1r[:, tile, :], ALU.add)
                        ins.then_inc(sem(f"proj_free{j % 2}"), 1)
                        job_done(dve, t, j)
                        own(nc.vector.bn_stats(st[:, 6 * tile:6 * tile + 6], z2[:, tile, :]), solo=True)
                        own(nc.vector.bn_aggr(ag[:, 2 * tile:2 * tile + 2], st[:, 6 * tile:6 * tile + 6]))
                    nc.vector.tensor_scalar(ve[:, :], ag[:, :].rearrange("p (t m) -> p t m", m=2)[:, :, 1], EPS, None,
                                            ALU.add).then_inc(sem("sum2_done"), 1)
                    t.w(dve, "rstd2", 1, 1, t.c)
                    for tile in range(TT):
                        last = nc.vector.tensor_scalar(z2[:, tile, :], z2[:, tile, :], ag[:, 2 * tile:2 * tile + 1],
                                                       rs[:, tile:tile + 1], ALU.subtract, ALU.mult)
                    last.then_inc(sem("x2_done"), 1)
                CHAIN["links"] = n[0]

            VSUM = 2 + TOPK + 2
            OWN_A = H + 2 * 5 + VSUM
            OWN_F = OWN_A + VSUM + NP + 2 * TT
            turns(dve, body)
            assert CHAIN["links"] == OWN_F - OWN_A

            dve.wait_ge(sem("x2_stored"), 16 * B)
            e_small = [sp_[0], sp_[1], pp[0], pp[1]]
            e_disp = [scp[0][:, 0:512], scp[0][:, 512:1024], scp[1][:, 0:512], scp[1][:, 512:1024]]
            for u in range(U):
                last = nc.vector.memset(bd[u][:, :, :], 0.0)
            last.then_inc(sem("bd_zero"), 1)
            dve.wait_ge(sem("e_const"), 16 * 3)
            with dve.Fori(0, NT // U) as i:
                for u in range(U):
                    dve.wait_ge(sem("logit_pe"), i * U + u + 1)
                    src = e_small[u][:, 256:384].rearrange("p (g t) -> p g t", t=GT)
                    nc.vector.tensor_tensor(lg[u][:, :, :], src, tiet[:, :].unsqueeze(1).to_broadcast([P, 4, GT]),
                                            ALU.add).then_inc(sem("own_l"), 1)
                    dve.wait_ge(sem("own_l"), i * 2 * U + 2 * u + 1)
                    nc.vector.tensor_reduce(mx[u][:, :], lg[u][:, :, :], AX, ALU.max).then_inc(sem("own_l"), 1)
                    dve.wait_ge(sem("own_l"), i * 2 * U + 2 * u + 2)
                    dve.wait_ge(sem("pma_done"), i * U + 1)
                    nc.vector.tensor_tensor(pm[u][:, :, :], lg[u][:, :, :],
                                            mx[u][:, :].unsqueeze(2).to_broadcast([P, 4, GT]), ALU.is_equal)\
                        .then_inc(sem("perm_done"), 1)
                for u in range(U):
                    dve.wait_ge(sem("disp_pe"), i * U + u + 2)
                    dst = dtt[:, 1, :, bass.ts(i * U + u, 4)].rearrange("p s g -> p g s")
                    nc.vector.tensor_copy(dst, e_disp[2 * (u % 2) + 1].rearrange("p (g s) -> p g s", g=4))\
                        .then_inc(sem(f"disp_dve{u % 2}"), 1)
            for u in range(2):
                dve.wait_ge(sem(f"disp_act{u}"), NT // 2 + 1)
                dve.wait_ge(sem(f"disp_dve{u}"), NT // 2 + 1)
                dve.wait_ge(sem("pma_done"), NT + 1)
            for u in range(2):
                last = nc.vector.memset(hb[u][:, :, :], 0.0)
            last.then_inc(sem("hb_zero"), 1)
            nc.vector.memset(mx[0][:, :], 0.0).then_inc(sem("disp_done"), 2 * NT)
            with dve.Fori(0, NQ // 2) as i:
                for u in range(2):
                    dve.wait_ge(sem(f"hidden_done{u}"), i + 1)
                    nc.vector.tensor_copy(zz[u][:, 0:1], fbt[:, bass.ts(i * 2 + u, 1)]).then_inc(sem(f"fbs_done{u}"), 1)
                for u in range(2):
                    dve.wait_ge(sem(f"ffn2_full{u}"), i + 2)
                    dst = dtt[:, 1, :, :].rearrange("p s g -> p (s g)")[:, bass.ts(i * 2 + u, 512)]
                    nc.vector.tensor_copy(dst, e_disp[2 * u + 1]).then_inc(sem(f"ffn2_dve{u}"), 1)
            for u in range(2):
                dve.wait_ge(sem(f"ffn2_act{u}"), NQ // 2 + 1)
                dve.wait_ge(sem(f"ffn2_dve{u}"), NQ // 2 + 1)
            nc.vector.memset(ve3[0][:, :], 0.0).then_inc(sem("ffn_done"), 2 * NQ)
            with dve.Fori(0, NT // 2) as i:
                for u in range(2):
                    dve.wait_ge(sem(f"inter_pe{u}"), i + 1)
                    src = dtt[:, 1, :, bass.ts(i * 2 + u, 4)].rearrange("p s g -> p g s")
                    nc.vector.tensor_copy(gi[u][:, 1, :, :], src).then_inc(sem(f"gi_dve{u}"), 1)
                for u in range(2):
                    dve.wait_ge(sem(f"inter_pe{u}"), i + 2)
                    nc.vector.tensor_copy(it_[u][:, 2:4, :].rearrange("p g d -> p (g d)"), e_disp[2 * u + 1])\
                        .then_inc(sem(f"inter_dve{u}"), 1)
                for u in range(2):
                    dve.wait_ge(sem(f"comb_pe{u}"), i + 2)
                    dve.wait_ge(sem(f"xc_in{u}"), i * 16 + 16)
                    nc.vector.tensor_tensor(zz[u][:, :], pp[u][:, 0:D], xc[u][:, :], ALU.add).then_inc(sem(f"sum3_{u}"), 1)
                    dve.wait_ge(sem(f"sum3_{u}"), i + 2)
                    nc.vector.bn_stats(st3[u][:, :], zz[u][:, :]).then_inc(sem(f"own_s{u}"), 1)
                    wait_apart(dve, f"own_s{u}", i * 2 + 1)
                    nc.vector.bn_aggr(ag3[u][:, :], st3[u][:, :]).then_inc(sem(f"own_s{u}"), 1)
                    dve.wait_ge(sem(f"own_s{u}"), i * 2 + 2)
                    nc.vector.tensor_scalar(ve3[u][:, :], ag3[u][:, 1:2], EPS, None, ALU.add).then_inc(sem(f"var3_{u}"), 1)
                for u in range(2):
                    dve.wait_ge(sem(f"rstd3_{u}"), i + 1)
                    nc.vector.tensor_scalar(oo[u][:, :], zz[u][:, :], ag3[u][:, 0:1], rs3[u][:, :], ALU.subtract, ALU.mult)\
                        .then_inc(sem(f"out_done{u}"), 1)

        @block.gpsimd
        def _(pool):
            prime(pool, "cm_lo", "ctx_lo")
            for n, (src, c, hi, lo) in enumerate(STAGES):
                pool.wait_ge(sem("stage_hi"), n + 1)
                nc.gpsimd.tensor_tensor(lo, stg[n % 2][:, :], hi.bitcast(F32), ALU.subtract)\
                    .then_inc(sem("stage_split"), 1)
            pool.wait_ge(sem("qz_zero"), 1)

            def gather(t, tile, batch):
                t.w(pool, "sum_done", TT, tile, batch)
                t.w(pool, "idx_done", TT, tile + 1, batch, apart=True)
                for k in range(TOPK):
                    pool.indirect_dma_start(out=vg[:, k, :], out_offset=None, in_=V_rows,
                                            in_offset=bass.IndirectOffsetOnAxis(ap=i8[:, tile, k:k + 1], axis=0))\
                        .then_inc(sem("vg_in"), 16)

            def rstd1(t, tile, batch):
                t.w(pool, "sum_done", TT, tile + 1, batch)
                nc.gpsimd.tensor_tensor(rs[:, 0:1], ve[:, 0:1], neghalf[:, 0:1], ALU.pow).then_inc(sem("rstd1"), 1)

            def body(t):
                if t.cross:
                    t.w(pool, "cm_hi", 1, 1, t.c)
                    nc.gpsimd.tensor_tensor(cml[:, :, :], cm[:, :, :], cmh[:, :, :].bitcast(F32), ALU.subtract)\
                        .then_inc(sem("cm_lo"), 1)
                    t.w(pool, "ctx_hi", 1, 1, t.c)
                    nc.gpsimd.tensor_tensor(ctl[:, :, :], ct[:, :, :], cth[:, :, :].bitcast(F32), ALU.subtract)\
                        .then_inc(sem("ctx_lo"), 1)
                    rstd1(t, 1, t.c)
                    t.w(pool, "x1_done", TT, TT, t.c)
                    for tile in range(TT):
                        last = nc.gpsimd.tensor_tensor(x1r[:, tile, :], x1[:, tile, :], bob[:, :], ALU.add)
                    last.then_inc(sem("x1r_done"), 1)
                for h in range(H):
                    if t.cross:
                        t.w(pool, "exp_done", H, h + 1, t.c, apart=True)
                        nc.gpsimd.tensor_scalar(ex[h % 4][:, :, :], ex[h % 4][:, :, :], E_LO, E_HI, ALU.max, ALU.min)\
                            .then_inc(sem("clip_done"), 1)
                    if t.attn and h == 8:
                        gather(t, 0, t.a)
                    if t.attn and h == 12:
                        rstd1(t, 0, t.a)
                if t.attn:
                    gather(t, 1, t.a)
                if t.cross:
                    t.w(pool, "sum2_done", 1, 1, t.c)
                    nc.gpsimd.tensor_tensor(rs[:, :], ve[:, :], neghalf[:, :], ALU.pow).then_inc(sem("rstd2"), 1)
                    t.w(pool, "x2_done", 1, 1, t.c)
                    pool.dma_start(x2_v[t.c], z2[:, :, :]).then_inc(sem("x2_stored"), 16)
                    t.w(pool, "x2_stored", 16, 16, t.c)

            turns(pool, body)
            pool.wait_ge(sem("x2_stored"), 16 * B)
            with pool.Fori(0, NT // 2) as i:
                for u in range(2):
                    pool.wait_ge(sem(f"var3_{u}"), i + 1)
                    nc.gpsimd.tensor_tensor(rs3[u][:, :], ve3[u][:, :], neghalf[:, 0:1], ALU.pow)\
                        .then_inc(sem(f"rstd3_{u}"), 1)
                for u in range(2):
                    pool.wait_ge(sem(f"out_done{u}"), i + 1)
                    pool.dma_start(out_t[i * 2 + u], oo[u][:, :]).then_inc(sem(f"out_stored{u}"), 16)
                for u in range(2):
                    pool.wait_ge(sem(f"out_stored{u}"), i * 16 + 16)


def kernel(**inp):
    import concourse.bacc as _bacc
    from concourse import mybir as _mybir
    from concourse.bass_utils import run_bass_kernel_spmd as _run

    def tiled(w):
        n = w.shape[1]
        return w.reshape(KT, P, n).transpose(1, 0, 2)

    a = {k: np.asarray(v) for k, v in inp.items()}
    x = a["x"].reshape(B * S, D)
    ctx = a["ctx_1024"].reshape(B * S, D)
    mask = a["mask_BxS2_bk1"]
    wkv = a["L0_xattn_Wkv"]
    bo = a["L0_xattn_bo"]
    off = np.stack([np.repeat(np.arange(NCH) * CH, 8), np.arange(NCH * 8)]).astype(np.float32)
    arrays = {
        "x": x,
        "xT": tiled(x.T),
        "ctxT": tiled(ctx.T),
        "mrow": np.broadcast_to(mask[:, None, :], (B, P, S)),
        "mcol": mask.reshape(B, KT, P).transpose(2, 1, 0),
        "A": a["L0_attn_A"],
        "AT": a["L0_attn_A"].T,
        "BmT": a["L0_attn_Bm"].T,
        "WimpT": a["L0_attn_W_imp"].T,
        "WrT": tiled(a["L0_attn_W_router"].T),
        "comp": a["L0_attn_compress"].reshape(NC, KT, P * R).transpose(1, 0, 2).reshape(P, P * R),
        "KmT": a["L0_attn_K"].T,
        "V": a["L0_attn_V"],
        "Wq": tiled(a["L0_xattn_Wq"]).reshape(P, KT * INNER),
        "Wk": tiled(wkv[:, :INNER]).reshape(P, KT * INNER),
        "Wv": tiled(wkv[:, INNER:]).reshape(P, KT * INNER),
        "Wo": a["L0_xattn_Wo"].reshape(NP, P, D).transpose(1, 0, 2),
        "bo": np.broadcast_to(bo[None, :], (P, D)),
        "ctrl": tiled(a["L0_ffn_controller"].reshape(D, SLOTS)),
        "f1": tiled(a["L0_ffn_f1"].reshape(D, SLOTS * F)),
        "fb": a["L0_ffn_bias"].reshape(NQ, P).T,
        "f2": a["L0_ffn_f2"].reshape(NQ, P, D),
        "ident": np.eye(P, dtype=np.float32),
        "tie": np.broadcast_to(np.linspace(0.0, 1e-6, GT, dtype=np.float32)[None], (P, GT)),
        "cidx": np.broadcast_to(off[None], (P, 2, NCH * 8)),
    }
    nc = _bacc.Bacc("TRN2", target_bir_lowering=False, num_devices=1)
    feed, args = {}, []
    for name, v in arrays.items():
        v = np.ascontiguousarray(v)
        feed[f"in_{name}"] = v
        args.append(nc.dram_tensor(f"in_{name}", v.shape, _mybir.dt.from_np(v.dtype), kind="ExternalInput").ap())
    o = nc.dram_tensor("out_x3", (B * S, D), _mybir.dt.float32, kind="ExternalOutput").ap()
    build(nc, *args, o)
    r = _run(nc, [feed], core_ids=[0])
    return r.results[0]["out_x3"].reshape(B, S, D)
```

```python
from contextlib import ExitStack

import numpy as np
import concourse.bass as bass
from concourse import mybir

F32 = mybir.dt.float32
F32R = mybir.dt.float32r
U32 = mybir.dt.uint32
U8 = mybir.dt.uint8
ALU = mybir.AluOpType
ACT = mybir.ActivationFunctionType
AX = mybir.AxisListType.X

P = 128
B, S, D = 16, 256, 256
KT = D // P
TT = S // P
SD = 64
NC = 64
R = 128
NK = 8192
TOPK = 8
STW = 1024
CH = 1024
NCH = NK // CH
H, DH = 16, 64
INNER = H * DH
NP = H // 2
GT = 32
SLOTS = 128
F = 32
NG = B * S // GT
NT = B * S // P
NQ = SLOTS // 4
RAD = 16
EPS = 1e-5
K_SCALE = float(R) ** -0.5
A_SCALE = float(DH) ** -0.5
E_LO, E_HI = float(np.exp(np.float32(-5.0))), float(np.exp(np.float32(5.0)))

PRE_PE = {k: n + 1 for n, k in enumerate(("scan1", "scan2", "hproj", "imp_pe", "impT_pe", "nw_pe", "nws_pe"))}
PRE_DVE = {k: n + 1 for n, k in enumerate(("scan1_evac", "scan2_evac", "hm_evac", "imp_max", "imp_sm", "uw_done",
                                           "nw_evac", "nd_done"))}

J_K, J_X1, J_Q, J_PV, J_V, J_WO, JOBS = 0, 4, 6, 10, 18, 22, 24


def build(nc, x, xT, ctxT, mrow, mcol, A, AT, BmT, WimpT, WrT, comp, KmT, V, Wq, Wk, Wv, Wo, bo, ctrl, f1, fb, f2,
          ident, tie, cidx, out):
    scd = nc.dram_tensor("shared_compress", [B * KT, P * R], F32, kind="Internal").ap()
    x2d = nc.dram_tensor("x2_scratch", [B * S, D], F32, kind="Internal").ap()
    with ExitStack() as ctx:
        names = {}

        def sem(name):
            if name not in names:
                names[name] = ctx.enter_context(nc.semaphore(name))
            return names[name]

        def sb(stack, name, shape, dt=F32):
            return stack.enter_context(nc.sbuf_tensor(name, shape, dt))

        def ps(name, cols):
            return ctx.enter_context(nc.psum_tensor(name, [P, cols], F32))

        scp = [ps(f"score_bank{i}", CH) for i in range(2)]
        sp_ = [ps(f"sim_bank{i}", 512) for i in range(2)]
        pp = [ps(f"proj_bank{i}", 512) for i in range(2)]

        idn = sb(ctx, "identity", [P, P])
        neghalf = sb(ctx, "neghalf", [P, 2])

        main = ctx.enter_context(ExitStack())
        kh, kl = sb(main, "keysT_hi", [P, NK], F32R), sb(main, "keysT_lo", [P, NK], F32R)
        wh, wl = sb(main, "wqkv_hi", [P, 3, KT, INNER], F32R), sb(main, "wqkv_lo", [P, 3, KT, INNER], F32R)
        wo = sb(main, "wo", [P, NP, D])
        bob = sb(main, "bo_bcast", [P, D])
        mcu = sb(main, "mask_col_u8", [P, KT, B], U8)
        mv = sb(main, "mask_weight", [P, KT, B])
        cix = sb(main, "chunk_offset", [P, 2, NCH * 8])

        pre = main.enter_context(ExitStack())
        xTa = sb(pre, "xT_all_", [P, KT, B * S])
        stg = [sb(pre, f"stage_{i}", [P, STW]) for i in range(2)]
        pw = sb(pre, "A_pow", [SD, RAD + 1, SD])
        qw = sb(pre, "A16_pow", [SD, RAD + 1, SD])
        tpw = [sb(pre, f"AT_pow{i}", [SD, SD]) for i in range(8)]
        bmt = sb(pre, "Bm_T", [SD, D])
        wit = sb(pre, "Wimp_T", [SD, D])
        wrt = sb(pre, "Wrouter_T", [P, KT, NC])
        ba = sb(pre, "Bm_A_pow", [P, KT, RAD, SD])
        gt = sb(pre, "scan_partial", [SD, B, RAD])
        ht = sb(pre, "h_final_T", [SD, B])
        hm = sb(pre, "h_proj_diag", [P, KT, B, B])
        impe = sb(pre, "importance", [B, S])
        imx = sb(pre, "imp_small", [B, 4])
        rte = sb(pre, "router_exp", [P, NT, NC])
        rmx = sb(pre, "router_max", [P, NT])
        rsm = sb(pre, "router_sum", [P, NT])
        uw = sb(pre, "token_weight", [P, NT])
        nw = sb(pre, "neuron_w", [NC, 3, B])
        ones = sb(pre, "ones64", [NC, NC])
        nd = sb(pre, "neuron_diag", [P, B, KT])
        cst = [sb(pre, f"comp_stage_{i}", [P, 512]) for i in range(5)]
        scs = [ba[0:B * KT, i // 2, (i % 2) * 8:(i % 2) * 8 + 8, :].rearrange("p a b -> p (a b)") for i in range(4)]
        pre.close()

        work = main.enter_context(ExitStack())
        xt = sb(work, "xT_in", [P, KT, S])
        xth, xtl = sb(work, "xT_hi", [P, KT, S], F32R), sb(work, "xT_lo", [P, KT, S], F32R)
        xn = sb(work, "x_in", [P, TT, D])
        sct = sb(work, "sc_in", [P, KT, R])
        sch, scl = sb(work, "sc_hi", [P, KT, R], F32R), sb(work, "sc_lo", [P, KT, R], F32R)
        qth, qtl = sb(work, "qT_hi", [P, S], F32R), sb(work, "qT_lo", [P, S], F32R)
        cv = sb(work, "cand_val", [P, TT, NCH * 8])
        ci = sb(work, "cand_idx", [P, TT, NCH * 8], U32)
        cf = sb(work, "cand_idx_f", [P, NCH * 8])
        v8 = sb(work, "top_val", [P, TT, TOPK])
        p8 = sb(work, "top_pos", [P, TOPK], U32)
        eqf = sb(work, "pos_onehot", [P, TOPK * NCH * 8])
        eq = eqf[:, :].rearrange("p (k c) -> p k c", k=TOPK)
        i8 = sb(work, "top_idx", [P, TT, TOPK], U32)
        nb = sb(work, "neg_max", [P, TT])
        w8 = sb(work, "top_weight", [P, TT, TOPK])
        wsum = sb(work, "weight_sum", [P, TT, 2])
        vg = sb(work, "v_rows", [P, TOPK, D])
        rd, acc = eqf[:, 0:S], eqf[:, S:S + D]
        st = sb(work, "ln_stats", [P, 6 * TT])
        ag = sb(work, "ln_aggr", [P, 2 * TT])
        ve = sb(work, "ln_var", [P, TT])
        rs = sb(work, "ln_rstd", [P, TT])
        x1 = sb(work, "x1", [P, TT, D])
        x1r = sb(work, "x1_residual", [P, TT, D])
        x1h, x1l = sb(work, "x1T_hi", [P, KT, S], F32R), sb(work, "x1T_lo", [P, KT, S], F32R)
        ct = sb(work, "ctxT_in", [P, KT, S])
        mr = sb(work, "mask_row", [P, S], U8)
        cm = sb(work, "ctxT_masked", [P, KT, S])
        cmh, cml = sb(work, "ctxm_hi", [P, KT, S], F32R), sb(work, "ctxm_lo", [P, KT, S], F32R)
        cth, ctl = sb(work, "ctx_hi", [P, KT, S], F32R), sb(work, "ctx_lo", [P, KT, S], F32R)
        kt = sb(work, "kT", [P, NP, S])
        qz = sb(work, "qT_padded", [P, H, S])
        vv = sb(work, "v", [P, KT, INNER])
        ms = sb(work, "mask_weight_next", [P, KT])
        mb = sb(work, "mask_weight_b", [P, KT, DH])
        ex = [sb(work, f"exp{i}", [P, KT, S]) for i in range(4)]
        ot = kt
        z2 = x1r
        main.close()

        exl = ctx.enter_context(ExitStack())
        U = 4
        dtt = sb(exl, "dispatchedT", [P, KT, SLOTS, NG])
        pma = sb(exl, "permT_all", [P, B * S])
        ctr = sb(exl, "controller", [P, KT, SLOTS])
        tiet = sb(exl, "tie", [P, GT])
        fbt = sb(exl, "ffn_bias", [P, NQ])
        f1q = [sb(exl, f"f1_quad{u}", [P, KT, P]) for u in range(U)]
        f2q = [sb(exl, f"f2_quad{u}", [P, D]) for u in range(U)]
        d1 = exl.enter_context(ExitStack())
        zero = sb(d1, "zeros", [P, 4 * SLOTS])
        xb = [sb(d1, f"x2_tile{u}", [P, D]) for u in range(U)]
        xbh = [sb(d1, f"x2_tile_hi{u}", [P, D], F32R) for u in range(U)]
        xbl = [sb(d1, f"x2_tile_lo{u}", [P, D], F32R) for u in range(U)]
        xbt = [sb(d1, f"x2T_tile{u}", [P, KT, P]) for u in range(U)]
        lg = [sb(d1, f"logits{u}", [P, 4, GT]) for u in range(U)]
        mx = [sb(d1, f"logit_max{u}", [P, 4]) for u in range(U)]
        pm = [sb(d1, f"permT{u}", [P, 4, GT]) for u in range(U)]
        bd = [sb(d1, f"perm_diag{u}", [P, 4, SLOTS], F32R) for u in range(U)]
        d1.close()
        d2 = exl.enter_context(ExitStack())
        gq = [sb(d2, f"dispatched_quad{u}", [P, KT, 4 * NG]) for u in range(U)]
        hb = [sb(d2, f"hidden_diag{u}", [P, 4, NG]) for u in range(U)]
        fbs = [sb(d2, f"bias_quad{u}", [P, 1]) for u in range(U)]
        d2.close()
        d3 = exl.enter_context(ExitStack())
        xc = [sb(d3, f"x2_again{u}", [P, D]) for u in range(U)]
        gi = [sb(d3, f"group_inter{u}", [P, KT, 4, SLOTS]) for u in range(U)]
        pms = [sb(d3, f"permT_static{u}", [P, P]) for u in range(U)]
        it_ = [sb(d3, f"inter{u}", [P, 4, D]) for u in range(U)]
        zz = [sb(d3, f"x3_sum{u}", [P, D]) for u in range(U)]
        st3 = [sb(d3, f"stats3_{u}", [P, 6]) for u in range(U)]
        ag3 = [sb(d3, f"aggr3_{u}", [P, 2]) for u in range(U)]
        ve3 = [sb(d3, f"var3_{u}", [P, 1]) for u in range(U)]
        rs3 = [sb(d3, f"rstd3_{u}", [P, 1]) for u in range(U)]
        oo = [sb(d3, f"out_tile{u}", [P, D]) for u in range(U)]
        d3.close()

        V_rows = V
        scd_v = scd.rearrange("(b k) (p r) -> b p k r", k=KT, r=R)
        xn_v = x.rearrange("(b t p) d -> b p t d", p=P, t=TT)
        x2_v = x2d.rearrange("(b t p) d -> b p t d", p=P, t=TT)
        x2_t = x2d.rearrange("(n p) d -> n p d", p=P)
        out_t = out.rearrange("(n p) d -> n p d", p=P)

        block = ctx.enter_context(nc.Block())

        spare = {}

        def wait_apart(eng, name, v):
            if not isinstance(v, int):
                if eng not in spare:
                    spare[eng] = eng.alloc_register("wait_value")
                eng.reg_mov(spare[eng], v)
                v = spare[eng]
            eng.wait_ge(sem("v_const"), 1)
            eng.wait_ge(sem(name), v)

        PRIMED = ("proj_free0", "proj_free1", "exp_done", "cm_lo", "ctx_lo")

        def prime(eng, *which):
            for name in which:
                eng.sem_inc(sem(name), 1)

        class Turn:

            def __init__(self, c):
                self.c, self.m, self.a, self.q = c, c + 1, c + 2, c + 3
                whole = not isinstance(c, int)
                self.cross, self.mid, self.attn, self.prep = (whole or 0 <= c + n < B for n in range(4))

            def w(self, eng, name, per, k, of, apart=False):
                v = of * per + k + (name in PRIMED)
                if isinstance(v, int) and v <= (name in PRIMED):
                    return
                if apart:
                    wait_apart(eng, name, v)
                else:
                    eng.wait_ge(sem(name), v)

        def turns(eng, body):
            for c in range(-3, 0):
                body(Turn(c))
            with eng.Fori(0, B - 3) as c:
                body(Turn(c))
            for c in range(B - 3, B):
                body(Turn(c))

        def uses(t, j):
            if isinstance(t.c, int) and t.c < 0:
                return j // 2 - J_V // 2 + JOBS // 2
            return j // 2 + 2 - (0 if t.mid or j < J_WO else 2)

        def job_free(eng, t, j):
            t.w(eng, f"proj_free{j % 2}", JOBS // 2, uses(t, j), t.c)

        def job_full(eng, t, j):
            t.w(eng, f"proj_full{j % 2}", JOBS // 2, uses(t, j) + 1, t.c)

        def job_done(eng, t, j):
            t.w(eng, f"proj_free{j % 2}", JOBS // 2, uses(t, j) + 1, t.c)

        class Step:

            def __init__(self, turn, u):
                self.turn, self.u = turn, u
                self.whole = not isinstance(turn, int)
                self.n = turn * U + u

            def has(self, k):
                return self.whole or 0 <= self.n + k < NT

            def buf(self, k):
                return (self.u + k) % U

            def at(self, k):
                return self.n + k

            def w(self, eng, name, k, per=1):
                v = (self.n + k + 1) * per
                if not isinstance(v, int) or v > 0:
                    eng.wait_ge(sem(name), v)

            def wbuf(self, eng, name, k, per=16):
                v = (self.turn + (self.u + k) // U + 1) * per
                if not isinstance(v, int) or v > 0:
                    eng.wait_ge(sem(f"{name}{self.buf(k)}"), v)

        def steps(eng, body):
            for n in range(-U, U):
                body(Step(n // U, n % U))
            with eng.Fori(1, NT // U - 1) as i:
                for u in range(U):
                    body(Step(i, u))
            for n in range(NT - U, NT + U):
                body(Step(n // U, n % U))

        sc_bank = [sp_[0], sp_[1], scp[0][:, 0:512], scp[0][:, 512:1024]]
        e_small = [sp_[0], sp_[1], pp[0], pp[1]]
        e_disp = [scp[0][:, 0:512], scp[0][:, 512:1024], scp[1][:, 0:512], scp[1][:, 512:1024]]

        def apart(eng):
            eng.wait_ge(sem("v_const"), 1)

        STAGES = [(KmT, c, kh[:, c * STW:(c + 1) * STW], kl[:, c * STW:(c + 1) * STW]) for c in range(NK // STW)]
        STAGES += [(w, k, wh[:, n, k, :], wl[:, n, k, :]) for n, w in enumerate((Wq, Wk, Wv)) for k in range(KT)]
        NCS = P * R // 512

        @block.sync
        def _(sp):
            for dst, src in ((pw[:, 1, :], A), (tpw[0][:, :], AT), (bmt[:, :], BmT), (wit[:, :], WimpT),
                             (pw[:, 0, :], ident[0:SD, 0:SD]), (qw[:, 0, :], ident[0:SD, 0:SD]), (idn[:, :], ident)):
                sp.dma_start(dst, src).then_inc(sem("small_in"), 16)
            for q in range(4):
                n = B * S // 4
                sp.dma_start(xTa[:, :, q * n:(q + 1) * n], xT[:, :, q * n:(q + 1) * n]).then_inc(sem("xTa_in"), 16)
            sp.dma_start(wrt[:, :, :], WrT).then_inc(sem("xTa_in"), 16)
            for n in range(5):
                sp.dma_start(cst[n][:, :], comp[:, n * 512:(n + 1) * 512]).then_inc(sem(f"comp_in{n}"), 16)
            for n in range(NCS):
                m = n + 4
                if 5 <= m < NCS:
                    sp.wait_ge(sem("comp_used"), m - 4)
                    sp.dma_start(cst[m % 5][:, :], comp[:, m * 512:(m + 1) * 512]).then_inc(sem(f"comp_in{m % 5}"), 16)
                sp.wait_ge(sem("sc_evac"), n + 1)
                sp.dma_start(scd[:, n * 512:(n + 1) * 512], scs[n % 4]).then_inc(sem(f"sc_store{n % 4}"), 16)
            for n in range(4):
                sp.wait_ge(sem(f"sc_store{n}"), 16 * NCS // 4)
            sp.wait_ge(sem("stage_split"), len(STAGES))
            sp.wait_ge(sem("stage_hi"), len(STAGES))

            def body(t):
                if t.prep:
                    t.w(sp, "x_lo", 1, 0, t.q)
                    sp.dma_start(xt[:, :, :], xT[:, :, bass.ts(t.q, S)]).then_inc(sem("xt_in"), 16)
                    t.w(sp, "sc_lo", 1, 0, t.q)
                    sp.dma_start(sct[:, :, :], scd_v[t.q]).then_inc(sem("sct_in"), 16)
                if t.mid:
                    t.w(sp, "ctx_lo", 1, 0, t.m)
                    sp.dma_start(ct[:, :, :], ctxT[:, :, bass.ts(t.m, S)]).then_inc(sem("ct_in"), 16)
                    sp.dma_start(mr[:, :], mrow[t.m]).then_inc(sem("mr_in"), 16)
                if t.attn:
                    t.w(sp, "sum_done", TT, 0, t.a)
                    sp.dma_start(xn[:, :, :], xn_v[t.a]).then_inc(sem("xn_in"), 16)

            turns(sp, body)

            sp.wait_ge(sem("x2_stored"), 16 * B)
            sp.dma_start(ctr[:, :, :], ctrl).then_inc(sem("e_const"), 16)
            sp.dma_start(tiet[:, :], tie).then_inc(sem("e_const"), 16)
            sp.dma_start(fbt[:, :], fb).then_inc(sem("e_const"), 16)

            def quad_load(t):
                if t.has(3):
                    t.w(sp, "ffn2_pe", -1)
                    u = t.buf(3)
                    sp.dma_start(f1q[u][:, :, :], f1[:, :, bass.ts(t.at(3), P)]).then_inc(sem(f"fq_in{u}"), 16)
                    sp.dma_start(f2q[u][:, :], f2[t.at(3)]).then_inc(sem(f"fq_in{u}"), 16)

            def tile_load(t):
                if t.has(3):
                    t.w(sp, "xbT_pe", -1)
                    t.w(sp, "x2_hi", -1)
                    t.w(sp, "x2_lo", -1)
                    u = t.buf(3)
                    sp.dma_start(xb[u][:, :], x2_t[t.at(3)]).then_inc(sem(f"xb_in{u}"), 16)

            def tile_again(t):
                if t.has(3):
                    t.w(sp, "sum3", -1)
                    u = t.buf(3)
                    sp.dma_start(xc[u][:, :], x2_t[t.at(3)]).then_inc(sem(f"xc_in{u}"), 16)

            steps(sp, tile_load)
            steps(sp, quad_load)
            sp.wait_ge(sem("ffn_done"), 1)
            steps(sp, tile_again)

        @block.tensor
        def _(pe):
            def mm(o, l, r, start=True, stop=True):
                return nc.tensor.matmul(o, l, r, start=start, stop=stop, skip_group_check=True)

            def mm3(o, lh, ll, rh, rl, first, last):
                mm(o, lh, rh, start=first, stop=False)
                mm(o, lh, rl, start=False, stop=False)
                return mm(o, ll, rh, start=False, stop=last)

            pe.wait_ge(sem("small_in"), 16 * 7)
            for r in range(8):
                if r:
                    pe.wait_ge(sem("pow_evac"), r)
                src, n = (pw, 1 << r) if r < 4 else (qw, 1 << (r - 4))
                m = 7 if r == 7 else n
                mm(scp[r % 2][0:SD, 0:m * SD], tpw[r][:, :], src[:, 1:1 + m, :].rearrange("p a b -> p (a b)"))
                last = mm(scp[r % 2][0:SD, 512:512 + SD], src[:, n, :], tpw[r][:, :])
                last.then_inc(sem("pow_pe"), 1)
            pe.wait_ge(sem("pow_evac"), 4)
            for n in range(4):
                k, hf = n // 2, n % 2
                if n >= 2:
                    pe.wait_ge(sem("ba_evac"), n - 1)
                mm(sp_[n % 2][:, :], bmt[:, k * P:(k + 1) * P],
                   pw[:, 8 * hf:8 * hf + 8, :].rearrange("p a b -> p (a b)")).then_inc(sem("ba_pe"), 1)
            pe.wait_ge(sem("ba_evac"), 4)
            pe.wait_ge(sem("xTa_in"), 16 * 5)
            for i in range(RAD):
                for k in range(KT):
                    last = mm(pp[0][0:SD, 0:B * RAD], ba[:, k, RAD - 1 - i, :],
                              xTa[:, k, :].rearrange("p (n i) -> p i n", i=RAD)[:, i, :],
                              start=(i == 0 and k == 0), stop=(i == RAD - 1 and k == KT - 1))
            last.then_inc(sem("pre_pe"), 1)
            for g in range(NT):
                if g % 8 == 0 and g >= 16:
                    pe.wait_ge(sem("router_evac"), g // 8 - 1)
                for k in range(KT):
                    last = mm(sp_[g // 8 % 2][:, (g % 8) * NC:(g % 8 + 1) * NC], xTa[:, k, g * P:(g + 1) * P],
                              wrt[:, k, :], start=(k == 0), stop=(k == KT - 1))
                if g % 8 == 7:
                    last.then_inc(sem("router_pe"), 1)
            pe.wait_ge(sem("pre_dve"), PRE_DVE["scan1_evac"])
            pe.wait_ge(sem("pow_evac"), 8)
            for j in range(RAD):
                last = mm(pp[1][0:SD, 0:B], qw[:, RAD - 1 - j, :], gt[:, :, j], start=(j == 0), stop=(j == RAD - 1))
            last.then_inc(sem("pre_pe"), 1)
            pe.wait_ge(sem("pre_dve"), PRE_DVE["scan2_evac"])
            for k in range(KT):
                last = mm(pp[1][:, 32 + k * B:32 + (k + 1) * B], wit[:, k * P:(k + 1) * P], ht[:, :])
            last.then_inc(sem("pre_pe"), 1)
            pe.wait_ge(sem("pre_dve"), PRE_DVE["hm_evac"])
            for b in range(B):
                for k in range(KT):
                    last = mm(pp[0][0:B, 0:S], hm[:, k, b, :], xTa[:, k, b * S:(b + 1) * S],
                              start=(b == 0 and k == 0), stop=(b == B - 1 and k == KT - 1))
            last.then_inc(sem("pre_pe"), 1)
            pe.wait_ge(sem("pre_dve"), PRE_DVE["imp_sm"])
            for t in range(TT):
                last = nc.tensor.transpose(pp[1][:, t * B:(t + 1) * B], impe[:, t * P:(t + 1) * P], idn[0:B, 0:B])
            last.then_inc(sem("pre_pe"), 1)
            pe.wait_ge(sem("pre_dve"), PRE_DVE["uw_done"])
            for b in range(B):
                for t in range(TT):
                    g = b * TT + t
                    last = mm(pp[0][0:NC, b:b + 1], rte[:, g, :], uw[:, g:g + 1], start=(t == 0), stop=(t == TT - 1))
            last.then_inc(sem("pre_pe"), 1)
            pe.wait_ge(sem("pre_dve"), PRE_DVE["nw_evac"])
            mm(pp[1][0:NC, 0:B], ones[:, :], nw[:, 0, :]).then_inc(sem("pre_pe"), 1)
            pe.wait_ge(sem("pre_dve"), PRE_DVE["nd_done"])
            for n in range(NCS):
                pe.wait_ge(sem(f"comp_in{n % 5}"), 16 * (n // 5 + 1))
                if n >= 4:
                    pe.wait_ge(sem("sc_evac"), n - 3)
                mm(sc_bank[n % 4][0:B * KT, :], nd[:, :, :].rearrange("p b k -> p (b k)"),
                   cst[n % 5][:, :]).then_inc(sem("comp_used"), 1)
            pe.wait_ge(sem("sc_evac"), 32)
            pe.wait_ge(sem("stage_split"), len(STAGES))
            pe.wait_ge(sem("stage_hi"), len(STAGES))
            pe.wait_ge(sem("main_const"), 16 * 4)
            pe.wait_ge(sem("qz_zero"), 1)

            def scores(t, h):
                tile, ch = h // NCH, h % NCH
                t.w(pe, "cand_done", H, h - 1, t.a)
                for n in range(CH // 512):
                    kc = slice(ch * CH + n * 512, ch * CH + (n + 1) * 512)
                    tc = slice(tile * P, (tile + 1) * P)
                    last = mm3(scp[h % 2][:, n * 512:(n + 1) * 512], qth[:, tc], qtl[:, tc], kh[:, kc], kl[:, kc],
                               True, True)
                last.then_inc(sem("score_full"), 1)

            def pv(t, p):
                j = J_PV + p
                t.w(pe, "clip_done", H, 2 * p + 2, t.c)
                job_free(pe, t, j)
                bank = pp[j % 2]
                for k in range(KT):
                    for o in range(2):
                        h = 2 * p + o
                        mm(bank[64 * o:64 * o + 64, 0:S], vv[:, k, h * DH:(h + 1) * DH], ex[h % 4][:, k, :],
                           start=(k == 0), stop=(k == KT - 1))
                for k in range(KT):
                    for o in range(2):
                        last = mm(bank[64 * o:64 * o + 64, S:2 * S], mb[:, k, :], ex[(2 * p + o) % 4][:, k, :],
                                  start=(k == 0), stop=(k == KT - 1))
                last.then_inc(sem(f"proj_full{j % 2}"), 1)

            def body(t):
                if t.cross:
                    t.w(pe, "cm_lo", 1, 1, t.c)
                    for m in range(4):
                        j = J_K + m
                        job_free(pe, t, j)
                        for o in range(2):
                            cs = slice((2 * m + o) * P, (2 * m + o + 1) * P)
                            for k in range(KT):
                                last = mm3(pp[j % 2][:, o * S:(o + 1) * S], wh[:, 1, k, cs], wl[:, 1, k, cs],
                                           cmh[:, k, :], cml[:, k, :], k == 0, k == KT - 1)
                        last.then_inc(sem(f"proj_full{j % 2}"), 1)
                    for tile in range(TT):
                        j = J_X1 + tile
                        t.w(pe, "x1_done", TT, tile + 1, t.c)
                        job_free(pe, t, j)
                        for k in range(KT):
                            last = nc.tensor.transpose(pp[j % 2][:, k * P:(k + 1) * P], x1[:, tile, k * P:(k + 1) * P],
                                                       idn[:, :])
                        last.then_inc(sem(f"proj_full{j % 2}"), 1)
                if t.attn:
                    t.w(pe, "q_lo", 1, 1, t.a)
                if t.cross:
                    for tile in range(TT):
                        job_done(pe, t, J_X1 + tile)
                    for m in range(4):
                        j = J_Q + m
                        job_free(pe, t, j)
                        for o in range(2):
                            cs = slice((2 * m + o) * P, (2 * m + o + 1) * P)
                            for k in range(KT):
                                last = mm3(pp[j % 2][:, o * S:(o + 1) * S], wh[:, 0, k, cs], wl[:, 0, k, cs],
                                           x1h[:, k, :], x1l[:, k, :], k == 0, k == KT - 1)
                        last.then_inc(sem(f"proj_full{j % 2}"), 1)
                for h in range(H):
                    if t.attn:
                        scores(t, h)
                    if t.cross:
                        if h == 0:
                            t.w(pe, "mb_done", 1, 1, t.c)
                        if h % 4 == 0:
                            job_done(pe, t, J_Q + h // 4)
                        t.w(pe, "exp_done", H, max(h - 1, 0), t.c)
                        for k in range(KT):
                            last = mm(sp_[h % 2][:, k * S:(k + 1) * S], kt[:, h // 2, k * P:(k + 1) * P], qz[:, h, :])
                        last.then_inc(sem("sim_full"), 1)
                        if h % 2 and h >= 3:
                            pv(t, (h - 3) // 2)
                if t.prep:
                    t.w(pe, "x_lo", 1, 1, t.q)
                    t.w(pe, "sc_lo", 1, 1, t.q)
                    if t.cross:
                        t.w(pe, "exp_done", H, H - 1, t.c)
                    for k in range(KT):
                        last = mm3(sp_[0][:, 0:S], sch[:, k, :], scl[:, k, :], xth[:, k, :], xtl[:, k, :],
                                   k == 0, k == KT - 1)
                    last.then_inc(sem("q_full"), 1)
                if t.cross:
                    pv(t, NP - 1)
                if t.mid:
                    t.w(pe, "ctx_lo", 1, 1, t.m)
                    for m in range(4):
                        j, tile, hf = J_V + m, m // 2, m % 2
                        job_free(pe, t, j)
                        for k in range(KT):
                            tc, cs = slice(tile * P, (tile + 1) * P), slice(hf * 512, (hf + 1) * 512)
                            last = mm3(pp[j % 2][:, :], cth[:, k, tc], ctl[:, k, tc], wh[:, 2, k, cs], wl[:, 2, k, cs],
                                       k == 0, k == KT - 1)
                        last.then_inc(sem(f"proj_full{j % 2}"), 1)
                if t.cross:
                    for tile in range(TT):
                        j = J_WO + tile
                        job_free(pe, t, j)
                        if tile == 0:
                            job_done(pe, t, J_PV + NP - 2)
                            job_done(pe, t, J_PV + NP - 1)
                        for p in range(NP):
                            last = mm(pp[j % 2][:, 0:D], ot[:, p, tile * P:(tile + 1) * P], wo[:, p, :],
                                      start=(p == 0), stop=(p == NP - 1))
                        last.then_inc(sem(f"proj_full{j % 2}"), 1)

            turns(pe, body)

            def select(t):
                if t.has(2):
                    u = t.buf(2)
                    t.wbuf(pe, "xb_in", 2)
                    t.w(pe, "bd_done", -2)
                    for k in range(KT):
                        last = nc.tensor.transpose(e_small[u][:, k * P:(k + 1) * P], xb[u][:, k * P:(k + 1) * P],
                                                   idn[:, :])
                    last.then_inc(sem("xbT_pe"), 1)
                if t.has(1):
                    u = t.buf(1)
                    t.w(pe, "xbT_evac", 1)
                    for k in range(KT):
                        last = mm(e_small[u][:, 256:384], ctr[:, k, :], xbt[u][:, k, :], start=(k == 0),
                                  stop=(k == KT - 1))
                    last.then_inc(sem("logit_pe"), 1)
                if t.has(0):
                    u = t.buf(0)
                    t.w(pe, "perm_done", 0)
                    nc.tensor.transpose(e_small[u][:, 384:512], pm[u][:, :, :].rearrange("p g t -> p (g t)"),
                                        idn[:, :]).then_inc(sem("perm_pe"), 1)
                if t.has(-1):
                    u = t.buf(-1)
                    t.w(pe, "bd_done", -1)
                    t.w(pe, "x2_lo", -1)
                    t.w(pe, "disp_act", -3)
                    t.w(pe, "disp_dve", -3)
                    rhs = bd[u][:, :, :].rearrange("p g s -> p (g s)")
                    for k in range(KT):
                        mm(e_disp[2 * (u % 2) + k], xbh[u][:, k * P:(k + 1) * P], rhs, True, False)
                        last = mm(e_disp[2 * (u % 2) + k], xbl[u][:, k * P:(k + 1) * P], rhs, False, True)
                    last.then_inc(sem("disp_pe"), 1)

            def ffn(t):
                if t.has(1):
                    u = t.buf(1)
                    t.wbuf(pe, "fq_in", 1, per=32)
                    t.w(pe, "quad_act", 1)
                    t.w(pe, "quad_dve", 1)
                    t.w(pe, "hidden_act", -3)
                    t.w(pe, "hidden_dve", -3)
                    for k in range(KT):
                        for s in range(4):
                            r = slice(F * s, F * (s + 1))
                            last = mm(e_small[u][r, 0:NG], f1q[u][:, k, r], gq[u][:, k, s * NG:(s + 1) * NG],
                                      start=(k == 0), stop=(k == KT - 1))
                    last.then_inc(sem("ffn1_pe"), 1)
                if t.has(0):
                    u = t.buf(0)
                    t.w(pe, "hidden_act", 0)
                    t.w(pe, "hidden_dve", 0)
                    t.w(pe, "ffn2_act", -2)
                    t.w(pe, "ffn2_dve", -2)
                    for k in range(KT):
                        last = mm(e_disp[2 * (u % 2) + k], f2q[u][:, k * P:(k + 1) * P],
                                  hb[u][:, :, :].rearrange("p s g -> p (s g)"))
                    last.then_inc(sem("ffn2_pe"), 1)

            def combine(t):
                if t.has(1):
                    u = t.buf(1)
                    t.w(pe, "regroup", 1, per=2)
                    t.w(pe, "inter_act", -1)
                    t.w(pe, "inter_dve", -1)
                    for g in range(4):
                        for k in range(KT):
                            c0 = (g % 2) * D + k * P
                            last = nc.tensor.transpose(e_disp[2 * (u % 2) + g // 2][:, c0:c0 + P], gi[u][:, k, g, :],
                                                       idn[:, :])
                    last.then_inc(sem("inter_pe"), 1)
                if t.has(0):
                    u = t.buf(0)
                    t.w(pe, "inter_act", 0)
                    t.w(pe, "inter_dve", 0)
                    t.w(pe, "perm_again", 0)
                    t.w(pe, "sum3", -4)
                    for g in range(4):
                        last = mm(e_small[u][GT * g:GT * (g + 1), 0:D], pms[u][:, GT * g:GT * (g + 1)], it_[u][:, g, :])
                    last.then_inc(sem("comb_pe"), 1)

            pe.wait_ge(sem("e_const"), 16 * 3)
            pe.wait_ge(sem("bd_zero"), U)
            steps(pe, select)
            pe.wait_ge(sem("disp_act"), NT)
            pe.wait_ge(sem("disp_dve"), NT)
            pe.wait_ge(sem("disp_done"), U)
            steps(pe, ffn)
            pe.wait_ge(sem("ffn2_act"), NT)
            pe.wait_ge(sem("ffn2_dve"), NT)
            steps(pe, combine)

        @block.scalar
        def _(act):
            prime(act, "proj_free0", "proj_free1", "exp_done")
            for n, (src, c, hi, lo) in enumerate(STAGES):
                if n >= 2:
                    act.wait_ge(sem("stage_split"), n - 1)
                    act.wait_ge(sem("stage_hi"), n - 1)
                act.dma_start(stg[n % 2][:, :], src[:, c * STW:(c + 1) * STW]).then_inc(sem(f"stage_in{n % 2}"), 16)
                if n >= 1:
                    m = n - 1
                    act.wait_ge(sem(f"stage_in{m % 2}"), 16 * (m // 2 + 1))
                    nc.scalar.copy(STAGES[m][2], stg[m % 2][:, :]).then_inc(sem("stage_hi"), 1)
            m = len(STAGES) - 1
            act.wait_ge(sem(f"stage_in{m % 2}"), 16 * (m // 2 + 1))
            nc.scalar.copy(STAGES[m][2], stg[m % 2][:, :]).then_inc(sem("stage_hi"), 1)
            for dst, src in ((wo[:, :, :], Wo), (bob[:, :], bo), (cix[:, :, :], cidx), (mcu[:, :, :], mcol)):
                act.dma_start(dst, src).then_inc(sem("main_const"), 16)
            for n in range(4):
                act.wait_ge(sem("router_sub"), n + 1)
                nc.scalar.activation(rte[:, 8 * n:8 * n + 8, :], rte[:, 8 * n:8 * n + 8, :], ACT.Exp)\
                    .then_inc(sem("router_exp"), 1)
            act.wait_ge(sem("pre_dve"), PRE_DVE["imp_max"])
            nc.scalar.activation(impe[:, :], pp[0][0:B, 0:S], ACT.Exp, bias=imx[:, 0:1], accum_out=imx[:, 1:2])\
                .then_inc(sem("imp_exp"), 1)
            for n in range(NCS):
                act.wait_ge(sem("comp_used"), n + 1)
                if n >= 4:
                    act.wait_ge(sem(f"sc_store{n % 4}"), 16 * (n // 4))
                nc.scalar.copy(scs[n % 4], sc_bank[n % 4][0:B * KT, :]).then_inc(sem("sc_evac"), 1)
            act.wait_ge(sem("stage_split"), len(STAGES))
            for n in range(4):
                act.wait_ge(sem(f"sc_store{n}"), 16 * NCS // 4)

            def weights8(t, tile, batch):
                t.w(act, "idx_done", TT, tile + 1, batch)
                nc.scalar.activation(w8[:, tile, :], v8[:, tile, :], ACT.Exp, bias=nb[:, tile:tile + 1], scale=K_SCALE,
                                     accum_out=wsum[:, tile, 0:1]).then_inc(sem("w8_exp"), 1)

            def body(t):
                if t.cross:
                    for m in range(4):
                        j = J_K + m
                        job_full(act, t, j)
                        nc.scalar.copy(kt[:, 2 * m:2 * m + 2, :].rearrange("p a s -> p (a s)"), pp[j % 2][:, :])\
                            .then_inc(sem(f"proj_free{j % 2}"), 1)
                    for tile in range(TT):
                        j = J_X1 + tile
                        job_full(act, t, j)
                        nc.scalar.copy(x1h[:, :, tile * P:(tile + 1) * P],
                                       pp[j % 2][:, 0:D].rearrange("p (k s) -> p k s", k=KT)).then_inc(sem("x1_hi"), 1)
                    for m in range(4):
                        j = J_Q + m
                        job_full(act, t, j)
                        for o in range(2):
                            r = slice(64 * o, 64 * o + 64)
                            last = nc.scalar.copy(
                                qz[r, 4 * m:4 * m + 4, :].rearrange("p (a o) s -> p a o s", o=2)[:, :, o, :],
                                pp[j % 2][r, :].rearrange("p (a s) -> p a s", a=2))
                        last.then_inc(sem(f"proj_free{j % 2}"), 1)
                for h in range(H):
                    if t.cross:
                        t.w(act, "sim_full", H, h + 1, t.c)
                        p = (h - 4) // 2
                        if p >= 0:
                            job_full(act, t, J_PV + p)
                        nc.scalar.activation(ex[h % 4][:, :, :].rearrange("p k s -> p (k s)"), sp_[h % 2][:, :],
                                             ACT.Exp, scale=A_SCALE).then_inc(sem("exp_done"), 1)
                    if t.mid and h == 0:
                        weights8(t, 1, t.m)
                    if t.attn and h == 12:
                        weights8(t, 0, t.a)
                    if t.prep and h == 3:
                        t.w(act, "xt_in", 16, 16, t.q)
                        t.w(act, "q_full", 1, 0, t.q)
                        nc.scalar.copy(xth[:, :, :], xt[:, :, :]).then_inc(sem("x_hi"), 1)
                        t.w(act, "sct_in", 16, 16, t.q)
                        nc.scalar.copy(sch[:, :, :], sct[:, :, :]).then_inc(sem("sc_hi"), 1)
                    if t.mid and h == 5:
                        t.w(act, "cm_done", 1, 1, t.m)
                        nc.scalar.copy(cmh[:, :, :], cm[:, :, :]).then_inc(sem("cm_hi"), 1)
                        nc.scalar.copy(cth[:, :, :], ct[:, :, :]).then_inc(sem("ctx_hi"), 1)
                if t.prep:
                    t.w(act, "q_full", 1, 1, t.q)
                    nc.scalar.copy(qth[:, :], sp_[0][:, 0:S]).then_inc(sem("q_hi"), 1)
                if t.mid:
                    for m in range(4):
                        j = J_V + m
                        job_full(act, t, j)
                        nc.scalar.mul(vv[:, m // 2, 512 * (m % 2):512 * (m % 2) + 512], pp[j % 2][:, :],
                                      ms[:, m // 2:m // 2 + 1]).then_inc(sem(f"proj_free{j % 2}"), 1)

            turns(act, body)

            def select(t):
                if t.has(2):
                    u = t.buf(2)
                    t.w(act, "xbT_pe", 2)
                    t.w(act, "logit_pe", -2)
                    nc.scalar.copy(xbt[u][:, :, :].rearrange("p k s -> p (k s)"), e_small[u][:, 0:256])\
                        .then_inc(sem("xbT_evac"), 1)
                    t.w(act, "disp_pe", -2)
                    t.w(act, "x2_lo", -2)
                    nc.scalar.copy(xbh[u][:, :], xb[u][:, :]).then_inc(sem("x2_hi"), 1)
                if t.has(0):
                    u = t.buf(0)
                    t.w(act, "perm_pe", 0)
                    t.w(act, "disp_pe", -4)
                    for g in range(4):
                        r = slice(GT * g, GT * (g + 1))
                        last = nc.scalar.copy(bd[u][r, g, :], e_small[u][r, 384:512])
                    last.then_inc(sem("bd_done"), 1)
                if t.has(-1):
                    apart(act)
                    t.w(act, "disp_pe", -1)
                    dst = dtt[:, 0, :, bass.ts(t.at(-1), 4)].rearrange("p s g -> p g s")
                    nc.scalar.copy(dst, e_disp[2 * (t.buf(-1) % 2)].rearrange("p (g s) -> p g s", g=4))\
                        .then_inc(sem("disp_act"), 1)

            def ffn(t):
                if t.has(2):
                    apart(act)
                    t.w(act, "ffn1_pe", -2)
                    src = dtt[:, 0, :, :].rearrange("p s g -> p (s g)")[:, bass.ts(t.at(2), 4 * NG)]
                    nc.scalar.copy(gq[t.buf(2)][:, 0, :], src).then_inc(sem("quad_act"), 1)
                if t.has(0):
                    u = t.buf(0)
                    t.w(act, "ffn1_pe", 0)
                    t.w(act, "ffn2_pe", -4)
                    t.w(act, "bias_done", 0)
                    for s in range(2):
                        r = slice(F * s, F * (s + 1))
                        last = nc.scalar.activation(hb[u][r, s, :], e_small[u][r, 0:NG], ACT.Relu, bias=fbs[u][r, 0:1])
                    last.then_inc(sem("hidden_act"), 1)
                if t.has(-1):
                    apart(act)
                    t.w(act, "ffn2_pe", -1)
                    dst = dtt[:, 0, :, :].rearrange("p s g -> p (s g)")[:, bass.ts(t.at(-1), 4 * NG)]
                    nc.scalar.copy(dst, e_disp[2 * (t.buf(-1) % 2)]).then_inc(sem("ffn2_act"), 1)

            def combine(t):
                if t.has(2):
                    u = t.buf(2)
                    apart(act)
                    t.w(act, "inter_pe", -2)
                    for k in range(KT):
                        src = dtt[:, k, :, bass.ts(t.at(2), 4)].rearrange("p s g -> p g s")
                        nc.scalar.copy(gi[u][:, k, :, :], src).then_inc(sem("regroup"), 1)
                    apart(act)
                    t.w(act, "comb_pe", -2)
                    nc.scalar.copy(pms[u][:, :], pma[:, bass.ts(t.at(2), P)]).then_inc(sem("perm_again"), 1)
                if t.has(1):
                    u = t.buf(1)
                    t.w(act, "inter_pe", 1)
                    t.w(act, "comb_pe", -3)
                    nc.scalar.copy(it_[u][:, 0:2, :].rearrange("p g d -> p (g d)"), e_disp[2 * (u % 2)])\
                        .then_inc(sem("inter_act"), 1)

            act.wait_ge(sem("x2_stored"), 16 * B)
            act.wait_ge(sem("zeros"), 1)
            for u in range(U):
                nc.scalar.copy(bd[u][:, :, :].rearrange("p g s -> p (g s)"), zero[:, :]).then_inc(sem("bd_zero"), 1)
            act.wait_ge(sem("bd_zero"), U)
            steps(act, select)
            act.wait_ge(sem("disp_done"), U)
            steps(act, ffn)
            act.wait_ge(sem("ffn_done"), 1)
            steps(act, combine)

        @block.vector
        def _(dve):
            def after(name, ins, n):
                ins.then_inc(sem(name), 1)
                dve.wait_ge(sem(name), n)

            nc.vector.memset(neghalf[:, :], -0.5).then_inc(sem("v_const"), 1)
            nc.vector.memset(ones[:, :], 1.0).then_inc(sem("v_const"), 1)
            after("v_const", nc.vector.memset(hm[:, :, :, :], 0.0), 3)
            after("v_const", nc.vector.memset(nd[:, :, :], 0.0), 4)
            for r in range(8):
                dve.wait_ge(sem("pow_pe"), r + 1)
                dst, n = (pw, 1 << r) if r < 4 else (qw, 1 << (r - 4))
                m = 7 if r == 7 else n
                last = nc.vector.tensor_copy(dst[:, n + 1:n + 1 + m, :].rearrange("p a b -> p (a b)"),
                                             scp[r % 2][0:SD, 0:m * SD])
                if r < 7:
                    last = nc.vector.tensor_copy(tpw[r + 1][:, :], scp[r % 2][0:SD, 512:512 + SD])
                if r == 3:
                    last = nc.vector.tensor_copy(qw[:, 1, :], scp[r % 2][0:SD, 7 * SD:8 * SD])
                last.then_inc(sem("pow_evac"), 1)
            for n in range(4):
                dve.wait_ge(sem("ba_pe"), n + 1)
                nc.vector.tensor_copy(ba[:, n // 2, 8 * (n % 2):8 * (n % 2) + 8, :].rearrange("p a b -> p (a b)"),
                                      sp_[n % 2][:, :]).then_inc(sem("ba_evac"), 1)
            dve.wait_ge(sem("pre_pe"), PRE_PE["scan1"])
            nc.vector.tensor_copy(gt[:, :, :].rearrange("p b j -> p (b j)"), pp[0][0:SD, 0:B * RAD])\
                .then_inc(sem("pre_dve"), 1)
            for n in range(4):
                dve.wait_ge(sem("router_pe"), n + 1)
                src = sp_[n % 2][:, :].rearrange("p (g n) -> p g n", n=NC)
                after("router_max", nc.vector.tensor_reduce(rmx[:, 8 * n:8 * n + 8], src, AX, ALU.max), n + 1)
                nc.vector.tensor_tensor(rte[:, 8 * n:8 * n + 8, :], src,
                                        rmx[:, 8 * n:8 * n + 8].unsqueeze(2).to_broadcast([P, 8, NC]),
                                        ALU.subtract).then_inc(sem("router_sub"), 1)
                dve.wait_ge(sem("router_sub"), n + 1)
                nc.vector.tensor_copy(uw[:, 8 * n:8 * n + 8], rmx[:, 8 * n:8 * n + 8]).then_inc(sem("router_evac"), 1)
            dve.wait_ge(sem("pre_pe"), PRE_PE["scan2"])
            nc.vector.tensor_copy(ht[:, :], pp[1][0:SD, 0:B]).then_inc(sem("pre_dve"), 1)
            dve.wait_ge(sem("pre_pe"), PRE_PE["hproj"])
            for k in range(KT):
                last = nc.vector.tensor_copy(hm[:, k, :, :].rearrange("p a b -> p (a b)")[:, 0:B * B:B + 1],
                                             pp[1][:, 32 + k * B:32 + (k + 1) * B])
            last.then_inc(sem("pre_dve"), 1)
            for n in range(4):
                dve.wait_ge(sem("router_exp"), n + 1)
                nc.vector.tensor_reduce(rsm[:, 8 * n:8 * n + 8], rte[:, 8 * n:8 * n + 8, :], AX, ALU.add)\
                    .then_inc(sem("router_sum"), 1)
            dve.wait_ge(sem("router_sum"), 4)
            dve.wait_ge(sem("router_evac"), 4)
            after("router_rec", nc.vector.reciprocal(uw[:, :], rsm[:, :]), 1)
            dve.wait_ge(sem("pre_pe"), PRE_PE["imp_pe"])
            nc.vector.tensor_reduce(imx[:, 0:1], pp[0][0:B, 0:S], AX, ALU.max, negate=True)\
                .then_inc(sem("pre_dve"), 1)
            dve.wait_ge(sem("imp_exp"), 1)
            after("imp_rec", nc.vector.reciprocal(imx[:, 2:3], imx[:, 1:2]), 1)
            nc.vector.tensor_scalar(impe[:, :], impe[:, :], imx[:, 2:3], None, ALU.mult).then_inc(sem("pre_dve"), 1)
            dve.wait_ge(sem("pre_pe"), PRE_PE["impT_pe"])
            nc.vector.tensor_tensor(uw[:, :].rearrange("p (b t) -> p t b", t=TT), uw[:, :].rearrange("p (b t) -> p t b", t=TT),
                                    pp[1][:, 0:TT * B].rearrange("p (t b) -> p t b", t=TT), ALU.mult)\
                .then_inc(sem("pre_dve"), 1)
            dve.wait_ge(sem("pre_pe"), PRE_PE["nw_pe"])
            nc.vector.tensor_copy(nw[:, 0, :], pp[0][0:NC, 0:B]).then_inc(sem("pre_dve"), 1)
            dve.wait_ge(sem("pre_pe"), PRE_PE["nws_pe"])
            after("nw_chain", nc.vector.tensor_scalar(nw[:, 1, :], pp[1][0:NC, 0:B], 1e-8, None, ALU.add), 1)
            after("nw_chain", nc.vector.reciprocal(nw[:, 2, :], nw[:, 1, :]), 2)
            for k in range(KT):
                last = nc.vector.tensor_tensor(nd[k * NC:(k + 1) * NC, :, k], nw[:, 0, :], nw[:, 2, :], ALU.mult)
            last.then_inc(sem("pre_dve"), 1)
            dve.wait_ge(sem("stage_split"), len(STAGES))
            for n in range(4):
                dve.wait_ge(sem(f"sc_store{n}"), 16 * NCS // 4)
            dve.wait_ge(sem("main_const"), 16 * 4)
            after("mv_done", nc.vector.tensor_scalar(mv[:, :, :], mcu[:, :, :], E_LO, None, ALU.max), 1)
            nc.vector.memset(qz[:, :, :], 0.0).then_inc(sem("qz_zero"), 1)

            seen = [0]

            def body(t):
                n = [0]

                def own(ins, solo=False):
                    n[0] += 1
                    ins.then_inc(sem("own"), 1)
                    base = seen[0] if isinstance(t.c, int) else t.c * OWN + seen[0]
                    if solo:
                        wait_apart(dve, "own", base + n[0])
                    else:
                        dve.wait_ge(sem("own"), base + n[0])

                def merge_pick(tile, batch):
                    t.w(dve, "cand_done", H, NCH * (tile + 1), batch, apart=True)
                    own(nc.vector.max(v8[:, tile, :], cv[:, tile, :]), solo=True)
                    own(nc.vector.max_index(p8[:, :], v8[:, tile, :], cv[:, tile, :]))
                    own(nc.vector.tensor_tensor(cf[:, :], ci[:, tile, :], cix[:, 0, :], ALU.add))

                def merge_index(tile, batch):
                    own(nc.vector.tensor_tensor(eq, cix[:, 1, :].unsqueeze(1).to_broadcast([P, TOPK, NCH * 8]),
                                                p8[:, :].unsqueeze(2).to_broadcast([P, TOPK, NCH * 8]), ALU.is_equal))
                    own(nc.vector.tensor_tensor(eq, eq,
                                                cf[:, :].unsqueeze(1).to_broadcast([P, TOPK, NCH * 8]), ALU.mult))
                    nc.vector.tensor_scalar(nb[:, tile:tile + 1], v8[:, tile, 0:1], -K_SCALE, None, ALU.mult)
                    with nc.allow_low_precision(reason="one index below 2^24 and zeros: exact"):
                        nc.vector.tensor_reduce(i8[:, tile, :], eq, AX, ALU.add).then_inc(sem("idx_done"), 1)
                    t.w(dve, "idx_done", TT, tile + 1, batch)

                def value_sum(tile, batch, ks):
                    if ks[0] == 0:
                        t.w(dve, "w8_exp", TT, tile + 1, batch)
                        own(nc.vector.reciprocal(wsum[:, tile, 1:2], wsum[:, tile, 0:1]))
                        own(nc.vector.tensor_scalar(w8[:, tile, :], w8[:, tile, :], wsum[:, tile, 1:2], None, ALU.mult))
                        t.w(dve, "xn_in", 16, 16, batch)
                        t.w(dve, "vg_in", 16 * TOPK * TT, 16 * TOPK * (tile + 1), batch)
                    for k in ks:
                        prev = xn[:, tile, :] if k == 0 else acc
                        own(nc.vector.scalar_tensor_tensor(acc, vg[:, k, :], w8[:, tile, k:k + 1], prev,
                                                           ALU.mult, ALU.add))
                    if ks[-1] != TOPK - 1:
                        return
                    own(nc.vector.bn_stats(st[:, 0:6], acc), solo=True)
                    own(nc.vector.bn_aggr(ag[:, 0:2], st[:, 0:6]))
                    nc.vector.tensor_scalar(ve[:, 0:1], ag[:, 1:2], EPS, None, ALU.add).then_inc(sem("sum_done"), 1)

                def value_norm(tile, batch):
                    t.w(dve, "rstd1", TT, tile + 1, batch)
                    t.w(dve, "x1r_done", 1, 0, batch)
                    nc.vector.tensor_scalar(x1[:, tile, :], acc, ag[:, 0:1], rs[:, 0:1], ALU.subtract, ALU.mult)\
                        .then_inc(sem("x1_done"), 1)

                def norm(p):
                    j = J_PV + p
                    if p:
                        job_done(dve, t, j - 1)
                    job_full(dve, t, j)
                    own(nc.vector.reciprocal(rd, pp[j % 2][:, S:2 * S]))
                    nc.vector.tensor_tensor(ot[:, p, :], pp[j % 2][:, 0:S], rd, ALU.mult)\
                        .then_inc(sem(f"proj_free{j % 2}"), 1)

                if t.cross:
                    nc.vector.tensor_copy(mb[:, :, :], mv[:, :, bass.ts(t.c, 1)].to_broadcast([P, KT, DH]))\
                        .then_inc(sem("mb_done"), 1)
                if t.mid:
                    merge_pick(1, t.m)
                    merge_index(1, t.m)
                if t.cross:
                    for tile in range(TT):
                        j = J_X1 + tile
                        t.w(dve, "x1_hi", TT, tile + 1, t.c)
                        nc.vector.tensor_tensor(x1l[:, :, tile * P:(tile + 1) * P],
                                                pp[j % 2][:, 0:D].rearrange("p (k s) -> p k s", k=KT),
                                                x1h[:, :, tile * P:(tile + 1) * P].bitcast(F32), ALU.subtract)\
                            .then_inc(sem(f"proj_free{j % 2}"), 1)
                if t.mid:
                    value_sum(0, t.m, range(TOPK))
                    value_norm(0, t.m)
                for h in range(H):
                    if t.attn:
                        tile, ch = h // NCH, h % NCH
                        t.w(dve, "score_full", H, h + 1, t.a, apart=True)
                        own(nc.vector.max(cv[:, tile, ch * 8:ch * 8 + 8], scp[h % 2][:, :]), solo=True)
                        nc.vector.max_index(ci[:, tile, ch * 8:ch * 8 + 8], cv[:, tile, ch * 8:ch * 8 + 8],
                                            scp[h % 2][:, :]).then_inc(sem("cand_done"), 1)
                    if t.mid and h == 2:
                        t.w(dve, "ct_in", 16, 16, t.m)
                        t.w(dve, "mr_in", 16, 16, t.m)
                        t.w(dve, "cm_lo", 1, 0, t.m)
                        nc.vector.tensor_tensor(cm[:, :, :], ct[:, :, :], mr[:, :].unsqueeze(1).to_broadcast([P, KT, S]),
                                                ALU.mult)
                        nc.vector.tensor_copy(ms[:, :], mv[:, :, t.m]).then_inc(sem("cm_done"), 1)
                    if t.prep and h == 4:
                        t.w(dve, "x_hi", 1, 1, t.q)
                        nc.vector.tensor_tensor(xtl[:, :, :], xt[:, :, :], xth[:, :, :].bitcast(F32), ALU.subtract)\
                            .then_inc(sem("x_lo"), 1)
                        t.w(dve, "sc_hi", 1, 1, t.q)
                        nc.vector.tensor_tensor(scl[:, :, :], sct[:, :, :], sch[:, :, :].bitcast(F32), ALU.subtract)\
                            .then_inc(sem("sc_lo"), 1)
                    if t.mid and h in (5, 6, 7):
                        value_sum(1, t.m, ((0, 1, 2), (3, 4, 5), (6, 7))[h - 5])
                    if t.mid and h == 9:
                        value_norm(1, t.m)
                        t.w(dve, "x1_done", TT, 2, t.m)
                    if t.attn and h == 8:
                        merge_pick(0, t.a)
                    if t.attn and h == 9:
                        merge_index(0, t.a)
                    if t.cross and h % 2 == 0 and h >= 4:
                        norm((h - 4) // 2)
                if t.cross:
                    norm(NP - 2)
                if t.prep:
                    t.w(dve, "q_hi", 1, 1, t.q)
                    nc.vector.tensor_tensor(qtl[:, :], sp_[0][:, 0:S], qth[:, :].bitcast(F32), ALU.subtract)\
                        .then_inc(sem("q_lo"), 1)
                if t.cross:
                    norm(NP - 1)
                    t.w(dve, "x1r_done", 1, 1, t.c)
                    for tile in range(TT):
                        j = J_WO + tile
                        job_full(dve, t, j)
                        ins = nc.vector.tensor_tensor(z2[:, tile, :], pp[j % 2][:, 0:D], x1r[:, tile, :], ALU.add)
                        ins.then_inc(sem(f"proj_free{j % 2}"), 1)
                        job_done(dve, t, j)
                        own(nc.vector.bn_stats(st[:, 6 * tile:6 * tile + 6], z2[:, tile, :]), solo=True)
                        own(nc.vector.bn_aggr(ag[:, 2 * tile:2 * tile + 2], st[:, 6 * tile:6 * tile + 6]))
                    nc.vector.tensor_scalar(ve[:, :], ag[:, :].rearrange("p (t m) -> p t m", m=2)[:, :, 1], EPS, None,
                                            ALU.add).then_inc(sem("sum2_done"), 1)
                    t.w(dve, "rstd2", 1, 1, t.c)
                    for tile in range(TT):
                        last = nc.vector.tensor_scalar(z2[:, tile, :], z2[:, tile, :], ag[:, 2 * tile:2 * tile + 1],
                                                       rs[:, tile:tile + 1], ALU.subtract, ALU.mult)
                    last.then_inc(sem("x2_done"), 1)
                if isinstance(t.c, int):
                    seen[0] += n[0]
                else:
                    assert n[0] == OWN
                    seen[0] += OWN * (B - 3)

            OWN = H + 2 * 5 + 2 * (2 + TOPK + 2) + NP + 2 * TT
            turns(dve, body)

            def select(t):
                if t.has(1):
                    u = t.buf(1)
                    t.w(dve, "logit_pe", 1)
                    t.w(dve, "perm_kept", -3)
                    src = e_small[u][:, 256:384].rearrange("p (g t) -> p g t", t=GT)
                    nc.vector.tensor_tensor(lg[u][:, :, :], src, tiet[:, :].unsqueeze(1).to_broadcast([P, 4, GT]),
                                            ALU.add).then_inc(sem("logits"), 1)
                    t.w(dve, "logits", 1)
                    nc.vector.tensor_reduce(mx[u][:, :], lg[u][:, :, :], AX, ALU.max).then_inc(sem("logit_max"), 1)
                    t.w(dve, "logit_max", 1)
                    t.w(dve, "perm_pe", -3)
                    nc.vector.tensor_tensor(pm[u][:, :, :], lg[u][:, :, :],
                                            mx[u][:, :].unsqueeze(2).to_broadcast([P, 4, GT]), ALU.is_equal)\
                        .then_inc(sem("perm_done"), 1)
                    apart(dve)
                    t.w(dve, "perm_done", 1)
                    nc.vector.tensor_copy(pma[:, bass.ts(t.at(1), P)], pm[u][:, :, :].rearrange("p g t -> p (g t)"))\
                        .then_inc(sem("perm_kept"), 1)
                if t.has(-1):
                    apart(dve)
                    t.w(dve, "disp_pe", -1)
                    dst = dtt[:, 1, :, bass.ts(t.at(-1), 4)].rearrange("p s g -> p g s")
                    nc.vector.tensor_copy(dst, e_disp[2 * (t.buf(-1) % 2) + 1].rearrange("p (g s) -> p g s", g=4))\
                        .then_inc(sem("disp_dve"), 1)

            def ffn(t):
                if t.has(2):
                    u = t.buf(2)
                    apart(dve)
                    t.w(dve, "ffn1_pe", -2)
                    src = dtt[:, 1, :, :].rearrange("p s g -> p (s g)")[:, bass.ts(t.at(2), 4 * NG)]
                    nc.vector.tensor_copy(gq[u][:, 1, :], src).then_inc(sem("quad_dve"), 1)
                    apart(dve)
                    t.w(dve, "hidden_act", -2)
                    t.w(dve, "hidden_dve", -2)
                    nc.vector.tensor_copy(fbs[u][:, :], fbt[:, bass.ts(t.at(2), 1)]).then_inc(sem("bias_done"), 1)
                if t.has(0):
                    u = t.buf(0)
                    t.w(dve, "ffn1_pe", 0)
                    t.w(dve, "ffn2_pe", -4)
                    t.w(dve, "bias_done", 0)
                    for s in range(2, 4):
                        r = slice(F * s, F * (s + 1))
                        last = nc.vector.tensor_scalar(hb[u][r, s, :], e_small[u][r, 0:NG], fbs[u][r, 0:1], 0.0,
                                                       ALU.add, ALU.max)
                    last.then_inc(sem("hidden_dve"), 1)
                if t.has(-1):
                    apart(dve)
                    t.w(dve, "ffn2_pe", -1)
                    dst = dtt[:, 1, :, :].rearrange("p s g -> p (s g)")[:, bass.ts(t.at(-1), 4 * NG)]
                    nc.vector.tensor_copy(dst, e_disp[2 * (t.buf(-1) % 2) + 1]).then_inc(sem("ffn2_dve"), 1)

            def combine(t):
                if t.has(1):
                    u = t.buf(1)
                    t.w(dve, "inter_pe", 1)
                    t.w(dve, "comb_pe", -3)
                    nc.vector.tensor_copy(it_[u][:, 2:4, :].rearrange("p g d -> p (g d)"), e_disp[2 * (u % 2) + 1])\
                        .then_inc(sem("inter_dve"), 1)
                if t.has(-1):
                    u = t.buf(-1)
                    t.w(dve, "comb_pe", -1)
                    t.wbuf(dve, "xc_in", -1)
                    t.w(dve, "out_done", -5)
                    nc.vector.tensor_tensor(zz[u][:, :], e_small[u][:, 0:D], xc[u][:, :], ALU.add)\
                        .then_inc(sem("sum3"), 1)
                    t.w(dve, "sum3", -1)
                    nc.vector.bn_stats(st3[u][:, :], zz[u][:, :]).then_inc(sem("stats3"), 1)
                    wait_apart(dve, "stats3", t.at(0))
                    nc.vector.bn_aggr(ag3[u][:, :], st3[u][:, :]).then_inc(sem("aggr3"), 1)
                    t.w(dve, "aggr3", -1)
                    nc.vector.tensor_scalar(ve3[u][:, :], ag3[u][:, 1:2], EPS, None, ALU.add).then_inc(sem("var3"), 1)
                if t.has(-2):
                    u = t.buf(-2)
                    t.w(dve, "rstd3", -2)
                    t.wbuf(dve, "out_stored", -6)
                    nc.vector.tensor_scalar(oo[u][:, :], zz[u][:, :], ag3[u][:, 0:1], rs3[u][:, :], ALU.subtract,
                                            ALU.mult).then_inc(sem("out_done"), 1)

            dve.wait_ge(sem("x2_stored"), 16 * B)
            nc.vector.memset(zero[:, :], 0.0).then_inc(sem("zeros"), 1)
            dve.wait_ge(sem("e_const"), 16 * 3)
            steps(dve, select)
            dve.wait_ge(sem("disp_act"), NT)
            dve.wait_ge(sem("disp_dve"), NT)
            dve.wait_ge(sem("perm_kept"), NT)
            for u in range(U):
                nc.vector.memset(hb[u][:, :, :], 0.0).then_inc(sem("disp_done"), 1)
            dve.wait_ge(sem("disp_done"), U)
            steps(dve, ffn)
            dve.wait_ge(sem("ffn2_act"), NT)
            dve.wait_ge(sem("ffn2_dve"), NT)
            nc.vector.memset(ve3[0][:, :], 0.0).then_inc(sem("ffn_done"), 1)
            dve.wait_ge(sem("ffn_done"), 1)
            steps(dve, combine)

        @block.gpsimd
        def _(pool):
            prime(pool, "cm_lo", "ctx_lo")
            for n, (src, c, hi, lo) in enumerate(STAGES):
                pool.wait_ge(sem("stage_hi"), n + 1)
                nc.gpsimd.tensor_tensor(lo, stg[n % 2][:, :], hi.bitcast(F32), ALU.subtract)\
                    .then_inc(sem("stage_split"), 1)
            pool.wait_ge(sem("qz_zero"), 1)

            def gather(t, tile, batch, ks):
                if ks[0] == 0:
                    t.w(pool, "sum_done", TT, tile, batch)
                    t.w(pool, "idx_done", TT, tile + 1, batch, apart=True)
                for k in ks:
                    pool.indirect_dma_start(out=vg[:, k, :], out_offset=None, in_=V_rows,
                                            in_offset=bass.IndirectOffsetOnAxis(ap=i8[:, tile, k:k + 1], axis=0))\
                        .then_inc(sem("vg_in"), 16)

            def rstd1(t, tile, batch):
                t.w(pool, "sum_done", TT, tile + 1, batch)
                nc.gpsimd.tensor_tensor(rs[:, 0:1], ve[:, 0:1], neghalf[:, 0:1], ALU.pow).then_inc(sem("rstd1"), 1)

            def body(t):
                if t.cross:
                    t.w(pool, "x1_done", TT, TT, t.c)
                    for tile in range(TT):
                        last = nc.gpsimd.tensor_tensor(x1r[:, tile, :], x1[:, tile, :], bob[:, :], ALU.add)
                    last.then_inc(sem("x1r_done"), 1)
                if t.mid:
                    rstd1(t, 0, t.m)
                for h in range(H):
                    if t.cross:
                        t.w(pool, "exp_done", H, h + 1, t.c, apart=True)
                        nc.gpsimd.tensor_scalar(ex[h % 4][:, :, :], ex[h % 4][:, :, :], E_LO, E_HI, ALU.max, ALU.min)\
                            .then_inc(sem("clip_done"), 1)
                    if t.mid and h < 4:
                        gather(t, 1, t.m, (2 * h, 2 * h + 1))
                    if t.attn and 10 <= h < 16:
                        g = (0, 1, 2, 4, 6, 7, 8)
                        gather(t, 0, t.a, range(g[h - 10], g[h - 9]))
                    if t.mid and h == 8:
                        rstd1(t, 1, t.m)
                    if t.mid and h == 7:
                        t.w(pool, "cm_hi", 1, 1, t.m)
                        nc.gpsimd.tensor_tensor(cml[:, :, :], cm[:, :, :], cmh[:, :, :].bitcast(F32), ALU.subtract)\
                            .then_inc(sem("cm_lo"), 1)
                    if t.mid and h == 9:
                        t.w(pool, "ctx_hi", 1, 1, t.m)
                        nc.gpsimd.tensor_tensor(ctl[:, :, :], ct[:, :, :], cth[:, :, :].bitcast(F32), ALU.subtract)\
                            .then_inc(sem("ctx_lo"), 1)
                if t.cross:
                    t.w(pool, "sum2_done", 1, 1, t.c)
                    nc.gpsimd.tensor_tensor(rs[:, :], ve[:, :], neghalf[:, :], ALU.pow).then_inc(sem("rstd2"), 1)
                    t.w(pool, "x2_done", 1, 1, t.c)
                    pool.dma_start(x2_v[t.c], z2[:, :, :]).then_inc(sem("x2_stored"), 16)
                    t.w(pool, "x2_stored", 16, 16, t.c)

            turns(pool, body)

            def select(t):
                if t.has(2):
                    u = t.buf(2)
                    t.w(pool, "x2_hi", 2)
                    t.w(pool, "disp_pe", -2)
                    nc.gpsimd.tensor_tensor(xbl[u][:, :], xb[u][:, :], xbh[u][:, :].bitcast(F32), ALU.subtract)\
                        .then_inc(sem("x2_lo"), 1)

            def combine(t):
                if t.has(-1):
                    u = t.buf(-1)
                    t.w(pool, "var3", -1)
                    nc.gpsimd.tensor_tensor(rs3[u][:, :], ve3[u][:, :], neghalf[:, 0:1], ALU.pow)\
                        .then_inc(sem("rstd3"), 1)
                if t.has(-2):
                    u = t.buf(-2)
                    t.w(pool, "out_done", -2)
                    pool.dma_start(out_t[t.at(-2)], oo[u][:, :]).then_inc(sem(f"out_stored{u}"), 16)

            pool.wait_ge(sem("x2_stored"), 16 * B)
            steps(pool, select)
            steps(pool, combine)
            for u in range(U):
                pool.wait_ge(sem(f"out_stored{u}"), 16 * NT // U)


def kernel(**inp):
    import concourse.bacc as _bacc
    from concourse import mybir as _mybir
    from concourse.bass_utils import run_bass_kernel_spmd as _run

    def tiled(w):
        n = w.shape[1]
        return w.reshape(KT, P, n).transpose(1, 0, 2)

    a = {k: np.asarray(v) for k, v in inp.items()}
    x = a["x"].reshape(B * S, D)
    ctx = a["ctx_1024"].reshape(B * S, D)
    mask = a["mask_BxS2_bk1"]
    wkv = a["L0_xattn_Wkv"]
    bo = a["L0_xattn_bo"]
    off = np.stack([np.repeat(np.arange(NCH) * CH, 8), np.arange(NCH * 8)]).astype(np.float32)
    arrays = {
        "x": x,
        "xT": tiled(x.T),
        "ctxT": tiled(ctx.T),
        "mrow": np.broadcast_to(mask[:, None, :], (B, P, S)),
        "mcol": mask.reshape(B, KT, P).transpose(2, 1, 0),
        "A": a["L0_attn_A"],
        "AT": a["L0_attn_A"].T,
        "BmT": a["L0_attn_Bm"].T,
        "WimpT": a["L0_attn_W_imp"].T,
        "WrT": tiled(a["L0_attn_W_router"].T),
        "comp": a["L0_attn_compress"].reshape(NC, KT, P * R).transpose(1, 0, 2).reshape(P, P * R),
        "KmT": a["L0_attn_K"].T,
        "V": a["L0_attn_V"],
        "Wq": tiled(a["L0_xattn_Wq"]).reshape(P, KT * INNER),
        "Wk": tiled(wkv[:, :INNER]).reshape(P, KT * INNER),
        "Wv": tiled(wkv[:, INNER:]).reshape(P, KT * INNER),
        "Wo": a["L0_xattn_Wo"].reshape(NP, P, D).transpose(1, 0, 2),
        "bo": np.broadcast_to(bo[None, :], (P, D)),
        "ctrl": tiled(a["L0_ffn_controller"].reshape(D, SLOTS)),
        "f1": tiled(a["L0_ffn_f1"].reshape(D, SLOTS * F)),
        "fb": a["L0_ffn_bias"].reshape(NQ, P).T,
        "f2": a["L0_ffn_f2"].reshape(NQ, P, D),
        "ident": np.eye(P, dtype=np.float32),
        "tie": np.broadcast_to(np.linspace(0.0, 1e-6, GT, dtype=np.float32)[None], (P, GT)),
        "cidx": np.broadcast_to(off[None], (P, 2, NCH * 8)),
    }
    nc = _bacc.Bacc("TRN2", target_bir_lowering=False, num_devices=1)
    feed, args = {}, []
    for name, v in arrays.items():
        v = np.ascontiguousarray(v)
        feed[f"in_{name}"] = v
        args.append(nc.dram_tensor(f"in_{name}", v.shape, _mybir.dt.from_np(v.dtype), kind="ExternalInput").ap())
    o = nc.dram_tensor("out_x3", (B * S, D), _mybir.dt.float32, kind="ExternalOutput").ap()
    build(nc, *args, o)
    r = _run(nc, [feed], core_ids=[0])
    return r.results[0]["out_x3"].reshape(B, S, D)
```
